# Optimizing a Trainium2 kernel written in Bass

```python
import numpy as np
import jax
import jax.numpy as jnp

def _softmax(x, axis=-1):
    return jax.nn.softmax(x, axis=axis)

def _gelu(x):
    return jax.nn.gelu(x, approximate=True)

def _silu(x):
    return jax.nn.silu(x)

def _sigmoid(x):
    return jax.nn.sigmoid(x)

def _layernorm(x, axis=-1, eps=1e-05):
    m = jnp.mean(x, axis=axis, keepdims=True)
    v = jnp.var(x, axis=axis, keepdims=True)
    return (x - m) / jnp.sqrt(v + eps)

def _scatter_add(tgt, idx, src, axis=0):
    return tgt.at[idx].add(src)

def _segment_sum(src, seg, n):
    return jax.ops.segment_sum(src, seg, n)
kernel_name = 'mk_decoder_postln_d1_seqx_r8_459dbf'

def setup_inputs(seed: int=0):
    np.random.seed(seed)
    _w = jnp.asarray

    def _rec_inputs():
        import jax
        import jax.numpy as jnp
        _rk = jax.random.key(seed)
        x = -0.000125 + 0.9999 * jax.random.normal(jax.random.fold_in(_rk, 1), (128, 64, 128), jnp.float32)
        _lenS = 64 - jax.random.randint(jax.random.fold_in(_rk, 7), (128,), 0, max(1, 64 // 4) + 1, jnp.int32)
        _lenS2 = 64 - jax.random.randint(jax.random.fold_in(_rk, 8), (128,), 0, max(1, 64 // 4) + 1, jnp.int32)
        _ctx_1024P = jax.random.normal(jax.random.fold_in(_rk, 11), (128, 16, 128), jnp.float32)
        _ctx_1024c = jax.random.dirichlet(jax.random.fold_in(_rk, 511), 0.3 * jnp.ones((16,), jnp.float32), (128, 64))
        _ctx_1024t = jnp.einsum('bsk,bkd->bsd', _ctx_1024c, _ctx_1024P)
        _ctx_1024t = _ctx_1024t * jax.lax.rsqrt(jnp.mean(jnp.square(_ctx_1024t)) + 1e-12) * 0.953939
        ctx_1024 = -1.52775e-05 + 0.999936 * (_ctx_1024t + 0.3 * jax.random.normal(jax.random.fold_in(_rk, 611), (128, 64, 128), jnp.float32))
        return (x, ctx_1024)
    x, ctx_1024 = _rec_inputs()

    def _L0_attn_setup():
        import jax, jax.numpy as jnp
        import numpy as np
        import math
        D_MODEL = 128
        key = jax.random.key(seed)
        ks = jax.random.split(key, 7)
        B, S, D = (4, 512, D_MODEL)
        s = 0.02
        return {'hidden_states': jax.random.normal(ks[0], (B, S, D), jnp.float32), 'Wq': jax.random.normal(ks[1], (D, D), jnp.float32) * s, 'bq': jnp.zeros((D,), jnp.float32), 'Wk': jax.random.normal(ks[2], (D, D), jnp.float32) * s, 'bk': jnp.zeros((D,), jnp.float32), 'Wv': jax.random.normal(ks[3], (D, D), jnp.float32) * s, 'bv': jnp.zeros((D,), jnp.float32)}
    _L0_attn_all = _L0_attn_setup()
    _L0_attn_in = {k: v for k, v in _L0_attn_all.items() if k in ('Wq', 'bq', 'Wk', 'bk', 'Wv', 'bv')}
    del _L0_attn_all

    def _L0_xattn_setup():
        import jax, jax.numpy as jnp
        import numpy as np
        from math import sqrt
        key = jax.random.key(seed)
        kq, kk, kv = jax.random.split(key, 3)
        B, S, D = (8, 512, 128)
        q = jax.random.normal(kq, (B, S, D), dtype=jnp.float32)
        k = jax.random.normal(kk, (B, S, D), dtype=jnp.float32)
        v = jax.random.normal(kv, (B, S, D), dtype=jnp.float32)
        return {'q': q, 'k': k, 'v': v}
    _L0_xattn_all = _L0_xattn_setup()
    _L0_xattn_in = {k: v for k, v in _L0_xattn_all.items() if k in ()}
    del _L0_xattn_all

    def _L0_ffn_setup():
        import jax, jax.numpy as jnp
        import numpy as np
        B, S, D, F, E, NS, K = (2, 128, 128, 512, 8, 8, 2)
        FS = F // NS
        key = jax.random.key(seed)
        ks = jax.random.split(key, 8)
        scale = 0.02
        return {'hidden_states': jax.random.normal(ks[0], (B, S, D), jnp.float32), 'gate_W': jax.random.normal(ks[1], (E, D), jnp.float32) * scale, 'w1_e': jax.random.normal(ks[2], (E, D, F), jnp.float32) * scale, 'w3_e': jax.random.normal(ks[3], (E, D, F), jnp.float32) * scale, 'w2_e': jax.random.normal(ks[4], (E, F, D), jnp.float32) * scale, 'w1_s': jax.random.normal(ks[5], (NS, D, FS), jnp.float32) * scale, 'w3_s': jax.random.normal(ks[6], (NS, D, FS), jnp.float32) * scale, 'w2_s': jax.random.normal(ks[7], (NS, FS, D), jnp.float32) * scale}
    _L0_ffn_all = _L0_ffn_setup()
    _L0_ffn_in = {k: v for k, v in _L0_ffn_all.items() if k in ('gate_W', 'w1_e', 'w3_e', 'w2_e', 'w1_s', 'w3_s', 'w2_s')}
    del _L0_ffn_all
    return {'x': x, 'ctx_1024': ctx_1024, 'L0_attn_Wq': _L0_attn_in['Wq'], 'L0_attn_bq': _L0_attn_in['bq'], 'L0_attn_Wk': _L0_attn_in['Wk'], 'L0_attn_bk': _L0_attn_in['bk'], 'L0_attn_Wv': _L0_attn_in['Wv'], 'L0_attn_bv': _L0_attn_in['bv'], 'L0_ffn_gate_W': _L0_ffn_in['gate_W'], 'L0_ffn_w1_e': _L0_ffn_in['w1_e'], 'L0_ffn_w3_e': _L0_ffn_in['w3_e'], 'L0_ffn_w2_e': _L0_ffn_in['w2_e'], 'L0_ffn_w1_s': _L0_ffn_in['w1_s'], 'L0_ffn_w3_s': _L0_ffn_in['w3_s'], 'L0_ffn_w2_s': _L0_ffn_in['w2_s']}

def reference(x, ctx_1024, L0_attn_Wq, L0_attn_bq, L0_attn_Wk, L0_attn_bk, L0_attn_Wv, L0_attn_bv, L0_ffn_gate_W, L0_ffn_w1_e, L0_ffn_w3_e, L0_ffn_w2_e, L0_ffn_w1_s, L0_ffn_w3_s, L0_ffn_w2_s):
    import jax
    import jax.numpy as jnp

    def _L0_attn_ref(hidden_states, Wq, bq, Wk, bk, Wv, bv):
        import jax, jax.numpy as jnp
        import numpy as np
        import math
        D_MODEL = 128
        D = hidden_states.shape[-1]
        scale = 1.0 / math.sqrt(D)
        q = hidden_states @ Wq.T + bq
        k = hidden_states @ Wk.T + bk
        v = hidden_states @ Wv.T + bv
        q = jax.nn.softmax(q, axis=-1)
        k = jax.nn.softmax(k, axis=-2) * scale
        v = jax.nn.softmax(v, axis=-2)
        attn = jnp.einsum('bqd,bkd->bqk', q, k)
        out = jnp.einsum('bqk,bkd->bqd', attn, v)
        return out

    def _L0_xattn_ref(q, k, v):
        import jax, jax.numpy as jnp
        import numpy as np
        from math import sqrt
        S = q.shape[1]
        scale = 1.0 / sqrt(S)
        qn = q * scale
        kn = k * scale
        kv_mat = jnp.einsum('bsd,bse->bde', kn, v)
        out = jnp.einsum('bsd,bde->bse', qn, kv_mat)
        return out

    def _L0_ffn_ref(hidden_states, gate_W, w1_e, w3_e, w2_e, w1_s, w3_s, w2_s):
        import jax, jax.numpy as jnp
        import numpy as np
        B, S, D, F, E, NS, K = (2, 128, 128, 512, 8, 8, 2)
        FS = F // NS
        b, s, d = hidden_states.shape
        e = gate_W.shape[0]
        flat = hidden_states.reshape(-1, d)
        T = flat.shape[0]
        logits = (flat @ gate_W.T).astype(jnp.float32)
        probs = jax.nn.softmax(logits, axis=-1)
        top_v, top_i = jax.lax.top_k(probs, K)
        gates = jnp.zeros((T, e), probs.dtype).at[jnp.arange(T)[:, None], top_i].set(top_v)
        g = jax.nn.silu(jnp.einsum('td,edf->etf', flat, w1_e))
        u = jnp.einsum('td,edf->etf', flat, w3_e)
        out_e = jnp.einsum('etf,efd->etd', g * u, w2_e)
        routed = jnp.einsum('te,etd->td', gates, out_e).reshape(b, s, d)
        gs = jax.nn.silu(jnp.einsum('bsd,ndf->nbsf', hidden_states, w1_s))
        us = jnp.einsum('bsd,ndf->nbsf', hidden_states, w3_s)
        shared = jnp.einsum('nbsf,nfd->bsd', gs * us, w2_s) / w1_s.shape[0]
        alpha = 0.5
        return alpha * shared + (1.0 - alpha) * routed
    x = _layernorm(x + _L0_attn_ref(x, L0_attn_Wq, L0_attn_bq, L0_attn_Wk, L0_attn_bk, L0_attn_Wv, L0_attn_bv), axis=-1)
    x = _layernorm(x + _L0_xattn_ref(x, ctx_1024, ctx_1024), axis=-1)
    x = _layernorm(x + _L0_ffn_ref(x, L0_ffn_gate_W, L0_ffn_w1_e, L0_ffn_w3_e, L0_ffn_w2_e, L0_ffn_w1_s, L0_ffn_w3_s, L0_ffn_w2_s), axis=-1)
    return x

_drawn_inputs = setup_inputs


def setup_inputs(seed=0):
    import zlib

    import numpy as np

    out = dict(_drawn_inputs(seed))
    spreads = {'L0_attn_bq': (0.0, 2.0), 'L0_attn_bk': (0.0, 2.0), 'L0_attn_bv': (0.0, 2.0)}
    factors = {'L0_attn_Wq': 48.088,
     'L0_attn_Wk': 57.869,
     'L0_attn_Wv': 54.44,
     'L0_ffn_gate_W': 8.0,
     'L0_ffn_w1_e': 8.0,
     'L0_ffn_w3_e': 8.0,
     'L0_ffn_w2_e': 8.0,
     'L0_ffn_w1_s': 8.0,
     'L0_ffn_w3_s': 8.0,
     'L0_ffn_w2_s': 8.0}
    for name, (base, spread) in spreads.items():
        noise = np.random.default_rng([zlib.crc32(name.encode()), seed]).standard_normal(out[name].shape)
        drawn = base * np.exp(spread * noise) if base else spread * noise
        out[name] = jnp.asarray(drawn.astype(out[name].dtype))
    for name, factor in factors.items():
        out[name] = (out[name] * factor).astype(out[name].dtype)
    return out
```

```python
from contextlib import ExitStack

import concourse.bass as bass
from concourse import mybir

F32 = mybir.dt.float32
BF16 = mybir.dt.bfloat16
I32 = mybir.dt.int32
U32 = mybir.dt.uint32
ACT = mybir.ActivationFunctionType
ALU = mybir.AluOpType
AX = mybir.AxisListType
ds = bass.ds

P = 128
B, S, D = 128, 64, 128
T = B * S
GT = 4
GN = GT * P
NG = T // GN
NT = T // P
GB = GN // S
E, F, K = 8, 512, 2
FC = F // P
NS, FS = 8, 64
SHARED = E
NB = T * K // P + E
EPS = 1e-5
Q_SCALE = float(D) ** -0.5
X_SCALE = 1.0 / S
ALPHA = 0.5
assert NS * FS == F and NB % 2 == 0 and NG % 2 == 0 and NT <= 256 and 2 * P <= 256 and NB <= 256


class Done:

    def __init__(self, engine, sem, before=0):
        self.engine, self.sem, self.before, self.n = engine, sem, before, 0

    def add(self, instruction):
        self.n += 1
        return instruction.then_inc(self.sem, 1)

    def wait(self):
        self.engine.wait_ge(self.sem, self.before + self.n)

    def link(self, instruction):
        self.add(instruction)
        self.wait()


class Turns:

    def __init__(self, engine, sem, name, first):
        self.engine, self.sem, self.count = engine, sem, engine.alloc_register(name)
        engine.reg_mov(self.count, first)

    def wait(self, value):
        if isinstance(value, int):
            self.engine.wait_ge(self.sem, value)
        else:
            self.engine.wait_ge(self.sem, self.engine.snap(self.count))
            self.engine.reg_add(self.count, self.count, 1)


def over(ap, n):
    return ap.unsqueeze(2).broadcast_to([ap.shape[0], ap.shape[1], n])


def across(ap, n):
    return ap.unsqueeze(1).broadcast_to([ap.shape[0], n, ap.shape[1]])


def decoder(nc, x, ctx, wq, bq, wk, bk, wv, bv, gate_w, w1_e, w3_e, w2_e, w1_s, w3_s, w2_s, out):
    stack = ExitStack()
    with stack:
        def sb(name, shape, dt=F32):
            return stack.enter_context(nc.sbuf_tensor(name, shape, dt))

        def sem(name):
            return stack.enter_context(nc.semaphore(name))

        bank = [stack.enter_context(nc.psum_tensor(f"bank{i}", [P, 512], F32)) for i in range(8)]

        x_rows = x.rearrange("b s d -> (b s) d")
        ctx_rows = ctx.rearrange("b s d -> (b s) d")
        out_rows = out.rearrange("b s d -> (b s) d")
        x2_rows = nc.dram_tensor("x2_rows", (T, D), F32, kind="Internal").ap()
        y_rows = nc.dram_tensor("y_rows", (T * K + NB * P, D), F32, kind="Internal").ap()

        def group_rows(rows, g):
            return rows[ds(g * GN, GN), :].rearrange("(j p) d -> p j d", p=P)

        w1 = sb("w1", [P, E + 1, F])
        w3 = sb("w3", [P, E + 1, F])
        w2 = sb("w2", [P, E + 1, FC * D])
        x2_all = sb("x2_all", [P, NT, D])
        x2T_all = sb("x2T_all", [P, T])
        ident = sb("ident", [P, P])
        top_v = sb("top_v", [P, NT, 8])
        top_i = sb("top_i", [P, NT, K])
        gates = sb("gates", [P, K, NT])
        src_tab = sb("src_tab", [P, NB], U32)
        dst_tab = sb("dst_tab", [P, NB], U32)
        w_at = sb("w_at", [P, NB], I32)
        minus_half = sb("minus_half", [P, 2 * GT])
        weights_in = sem("weights_in")

        attention(nc, sb, sem, bank, locals())
        routing(nc, sem, bank, locals())
        experts(nc, sem, bank, locals())
        combine(nc, sem, bank, locals())


def attention(nc, sb, sem, bank, m):
    bk, bv, bq, gate_w = m["bk"], m["bv"], m["bq"], m["gate_w"]
    group_rows, x_rows, ctx_rows, x2_rows = m["group_rows"], m["x_rows"], m["ctx_rows"], m["x2_rows"]
    w1, w3, w2, ident = m["w1"], m["w3"], m["w2"], m["ident"]
    x2_all, x2T_all, top_v, top_i = m["x2_all"], m["x2T_all"], m["top_v"], m["top_i"]
    minus_half, weights_in = m["minus_half"], m["weights_in"]
    stack = ExitStack()
    with stack:
        def sb(name, shape, dt=F32):
            return stack.enter_context(nc.sbuf_tensor(name, shape, dt))

        w_raw = sb("w_raw", [P, 3, D])
        gw_raw = sb("gw_raw", [E, D])
        wT = sb("wT", [P, 3, D])
        gwT = sb("gwT", [P, E])
        bq_row = sb("bq_row", [1, GT, D])
        ones_row = sb("ones_row", [1, P])
        bkv = sb("bkv", [P, 2])
        mask_a = sb("mask_a", [P, P])
        mask_x = sb("mask_x", [P, P])
        x_in = [sb(f"x_in{i}", [P, GT, D]) for i in range(2)]
        c_in = [sb(f"c_in{i}", [P, GT, D]) for i in range(2)]
        xT = sb("xT", [P, GN])
        cT = sb("cT", [P, GN])
        x1T = sb("x1T", [P, GN])
        x2T = [sb(f"x2T{i}", [P, GN]) for i in range(2)]
        eq = sb("eq", [P, GT, D])
        ek = sb("ek", [P, GB, S])
        ev = sb("ev", [P, GB, S])
        qT = sb("qT", [P, GN])
        vn = sb("vn", [P, GB, S])
        v = sb("v", [P, GT, D])
        sc_a = sb("sc_a", [P, GT, P])
        sc_x = sb("sc_x", [P, GT, P])
        y1 = sb("y1", [P, GT, D])
        y2 = sb("y2", [P, GT, D])
        x1 = [sb(f"x1_{i}", [P, GT, D]) for i in range(2)]
        x2 = [sb(f"x2_{i}", [P, GT, D]) for i in range(2)]
        nmax = sb("nmax", [P, GT])
        kvmax = sb("kvmax", [P, 2, GB])
        kvneg = sb("kvneg", [P, 2, GB])
        kvbias = sb("kvbias", [P, 2, GB])
        sums = sb("sums", [P, GT + 2 * GB])
        rsum = sb("rsum", [P, GT + 2 * GB])
        st = [sb(f"st{i}", [P, GT, 6]) for i in range(2)]
        mv = [sb(f"mv{i}", [P, GT, 2]) for i in range(2)]
        ve = [sb(f"ve{i}", [P, GT]) for i in range(2)]
        rs = [sb(f"rs{i}", [P, GT]) for i in range(2)]
        vs = sb("vs", [P, GT, 8])
        ix = sb("ix", [P, GT, 8], U32)

        small_in = sem("small_in")
        consts = sem("consts")
        wT_ps = sem("wT_ps")
        wT_ok = sem("wT_ok")
        x_ld = [sem(f"x_ld{i}") for i in range(2)]
        c_ld = [sem(f"c_ld{i}") for i in range(2)]
        stored = [sem(f"stored{i}") for i in range(2)]
        xT_ps = sem("xT_ps")
        xT_ok = sem("xT_ok")
        q_ps = sem("q_ps")
        k_ps = sem("k_ps")
        v_ps = sem("v_ps")
        qmax_ok = sem("qmax_ok")
        kvbias_ok = sem("kvbias_ok")
        eq_ok = sem("eq_ok")
        exps_ok = sem("exps_ok")
        rsum_ok = sem("rsum_ok")
        vn_ok = sem("vn_ok")
        qT_ps = sem("qT_ps")
        qT_ok = sem("qT_ok")
        vT_ps = sem("vT_ps")
        v_ok = sem("v_ok")
        sa_ps = sem("sa_ps")
        sa_ok = sem("sa_ok")
        o1_ps = sem("o1_ps")
        y1_ok = sem("y1_ok")
        ve1_ok = sem("ve1_ok")
        rs1_ok = sem("rs1_ok")
        x1_ok = sem("x1_ok")
        cT_ps = sem("cT_ps")
        cT_ok = sem("cT_ok")
        x1T_ps = sem("x1T_ps")
        x1T_ok = sem("x1T_ok")
        sx_ps = sem("sx_ps")
        sx_ok = sem("sx_ok")
        o2_ps = sem("o2_ps")
        y2_ok = sem("y2_ok")
        ve2_ok = sem("ve2_ok")
        rs2_ok = sem("rs2_ok")
        x2_ok = sem("x2_ok")
        x2T_ps = sem("x2T_ps")
        x2T_ok = sem("x2T_ok")
        l_ps = sem("l_ps")
        top_ok = sem("top_ok")
        st_ok = [sem(f"st_ok{n}") for n in range(2)]
        vs_ok = sem("vs_ok")
        dve_self = sem("dve_self")

        def tiles(b):
            return bank[b][:, :].rearrange("p (j n) -> p j n", j=GT)

        def batches(b):
            return bank[b][:, :].rearrange("p (j n) -> p j n", j=GB)

        def steps(engine, step):
            step(0, 0, 0, first=True, second=False, self_half=True, cross_half=False)
            step(1, 0, 1, first=False, second=True, self_half=True, cross_half=True)
            with engine.Fori(1, NG // 2) as j:
                for par in range(2):
                    step(j * 2 + par, j, par, first=False, second=False, self_half=True, cross_half=True)
            step(NG, NG // 2, 0, first=False, second=False, self_half=False, cross_half=True)

        block = stack.enter_context(nc.Block())

        @block.sync
        def _(sp):
            for n, w in enumerate((m["wq"], m["wk"], m["wv"])):
                sp.dma_start(w_raw[:, n, :], w).then_inc(small_in, 16)
            sp.dma_start(gw_raw[:, :], gate_w).then_inc(small_in, 16)
            for j in range(GT):
                sp.dma_start(bq_row[:, j, :], bq.rearrange("(a n) -> a n", a=1)).then_inc(small_in, 16)
            sp.dma_start(bkv[:, 0:1], bk.rearrange("(n a) -> n a", a=1)).then_inc(small_in, 16)
            sp.dma_start(bkv[:, 1:2], bv.rearrange("(n a) -> n a", a=1)).then_inc(small_in, 16)

            def store(h, hj, hp):
                sp.wait_ge(x2_ok, h + 1)
                sp.dma_start(group_rows(x2_rows, h), x2[hp][:, :, :]).then_inc(stored[hp], 16)
                sp.dma_start(x2_all[:, ds(h * GT, GT), :], x2[hp][:, :, :]).then_inc(stored[hp], 16)
                sp.wait_ge(x2T_ok, h + 1)
                sp.dma_start(x2T_all[:, ds(h * GN, GN)], x2T[hp][:, :]).then_inc(stored[hp], 16)

            def load(g, j, par, first):
                if not first:
                    sp.wait_ge(y1_ok, g - 1)
                sp.dma_start(x_in[par][:, :, :], group_rows(x_rows, g)).then_inc(x_ld[par], 16)
                if not first:
                    sp.wait_ge(o2_ps, g - 1)
                sp.dma_start(c_in[par][:, :, :], group_rows(ctx_rows, g)).then_inc(c_ld[par], 16)

            load(0, 0, 0, True)
            load(1, 0, 1, True)
            sp.dma_start(w1[:, 0:E, :], m["w1_e"].rearrange("e d f -> d e f")).then_inc(weights_in, 16)
            sp.dma_start(w3[:, 0:E, :], m["w3_e"].rearrange("e d f -> d e f")).then_inc(weights_in, 16)
            sp.dma_start(w1[:, SHARED, :].rearrange("d (n f) -> d n f", n=NS),
                         m["w1_s"].rearrange("n d f -> d n f")).then_inc(weights_in, 16)
            sp.dma_start(w3[:, SHARED, :].rearrange("d (n f) -> d n f", n=NS),
                         m["w3_s"].rearrange("n d f -> d n f")).then_inc(weights_in, 16)
            for e in range(E):
                sp.dma_start(w2[:, e, :].rearrange("p (c d) -> p c d", c=FC),
                             m["w2_e"][e].rearrange("(c p) d -> p c d", p=P)).then_inc(weights_in, 16)
            sp.dma_start(w2[:, SHARED, :].rearrange("p (c d) -> p c d", c=FC),
                         m["w2_s"].rearrange("n f d -> (n f) d").rearrange("(c p) d -> p c d", p=P)
                         ).then_inc(weights_in, 16)
            with sp.Fori(1, NG // 2) as j:
                for par in range(2):
                    load(j * 2 + par, j, par, False)
                    store(j * 2 + par - 2, j - 1, par)
            store(NG - 2, NG // 2 - 1, 0)
            store(NG - 1, NG // 2 - 1, 1)
            for par in range(2):
                sp.wait_ge(stored[par], 48 * (NG // 2))
            sp.wait_ge(weights_in, 16 * (5 + E))

        @block.gpsimd
        def _(pool):
            c = Done(pool, consts)
            c.add(nc.gpsimd.memset(ident[:, :], 0.0))
            c.add(nc.gpsimd.memset(ones_row[:, :], 1.0))
            c.add(nc.gpsimd.memset(minus_half[:, :], -0.5))
            for mask, value in ((mask_a, Q_SCALE), (mask_x, X_SCALE)):
                c.add(nc.gpsimd.memset(mask[:, :], 0.0))
                c.wait()
                c.link(nc.gpsimd.memset(mask[0:S, 0:S], value))
                c.link(nc.gpsimd.memset(mask[S:P, S:P], value))
            c.add(nc.gpsimd.affine_select(out=ident[:, :], in_=ident[:, :], compare_op=ALU.not_equal, fill=1.0,
                                          base=0, pattern=[[-1, P]], channel_multiplier=1))
            assert c.n == N_CONSTS

            def step(i, j, par, first, second, self_half, cross_half):
                g, h = i, i - 1
                if self_half:
                    pool.wait_ge(rsum_ok, g + 1)
                    nc.gpsimd.tensor_tensor(vn[:, :, :], ev[:, :, :], over(rsum[:, GT + GB:], S),
                                            ALU.mult).then_inc(vn_ok, 1)
                if cross_half:
                    pool.wait_ge(ve2_ok, h + 1)
                    nc.gpsimd.tensor_tensor(rs[1][:, :], ve[1][:, :], minus_half[:, 0:GT],
                                            ALU.pow).then_inc(rs2_ok, 1)
                if self_half:
                    pool.wait_ge(ve1_ok, g + 1)
                    nc.gpsimd.tensor_tensor(rs[0][:, :], ve[0][:, :], minus_half[:, 0:GT],
                                            ALU.pow).then_inc(rs1_ok, 1)

            steps(pool, step)

        @block.tensor
        def _(pe):
            pe.wait_ge(small_in, 16 * 10)
            pe.wait_ge(consts, N_CONSTS)
            for n in range(3):
                nc.tensor.transpose(bank[0][:, n * D:(n + 1) * D], w_raw[:, n, :], ident[:, :])
            nc.tensor.transpose(bank[0][:, 3 * D:3 * D + E], gw_raw[:, :], ident[0:E, 0:E]).then_inc(wT_ps, 1)
            pe.wait_ge(wT_ok, 1)

            def transposes(b, of):
                for t in range(GT):
                    last = nc.tensor.transpose(bank[b][:, t * P:(t + 1) * P], of(t), ident[:, :])
                return last

            def step(i, j, par, first, second, self_half, cross_half):
                g, h, hj, hp = i, i - 1, (j if par else j - 1), 1 - par
                if self_half:
                    pe.wait_ge(x_ld[par], 16 * (j + 1))
                    if not first:
                        pe.wait_ge(qT_ok, g)
                    transposes(0, lambda t: x_in[par][:, t, :]).then_inc(xT_ps, 1)
                if cross_half:
                    pe.wait_ge(c_ld[hp], 16 * (hj + 1))
                    if not second:
                        pe.wait_ge(top_ok, h)
                    transposes(4, lambda t: c_in[hp][:, t, :]).then_inc(cT_ps, 1)
                if self_half:
                    pe.wait_ge(xT_ok, g + 1)
                    if not first:
                        pe.wait_ge(v_ok, g)
                    nc.tensor.matmul(bank[1][:, :], ones_row[:, :], bq_row[:, :, :].rearrange("a j d -> a (j d)"),
                                     start=True, stop=False)
                    for t in range(GT):
                        last = nc.tensor.matmul(bank[1][:, t * P:(t + 1) * P], xT[:, t * P:(t + 1) * P],
                                                wT[:, 0, :], start=False, stop=(t == GT - 1))
                    last.then_inc(q_ps, 1)
                    if not first:
                        pe.wait_ge(sa_ok, g)
                    nc.tensor.matmul(bank[2][:, :], wT[:, 1, :], xT[:, :], start=True, stop=True).then_inc(k_ps, 1)
                    if not first:
                        pe.wait_ge(y1_ok, g)
                    nc.tensor.matmul(bank[3][:, :], wT[:, 2, :], xT[:, :], start=True, stop=True).then_inc(v_ps, 1)
                if cross_half:
                    pe.wait_ge(x1_ok, h + 1)
                    if not second:
                        pe.wait_ge(x2T_ok, h)
                    transposes(5, lambda t: x1[hp][:, t, :]).then_inc(x1T_ps, 1)
                    pe.wait_ge(cT_ok, h + 1)
                    pe.wait_ge(x1T_ok, h + 1)
                    if not second:
                        pe.wait_ge(sx_ok, h)
                    for t in range(GT):
                        last = nc.tensor.matmul(bank[6][:, t * P:(t + 1) * P], cT[:, t * P:(t + 1) * P],
                                                x1T[:, t * P:(t + 1) * P], start=True, stop=True)
                    last.then_inc(sx_ps, 1)
                if self_half:
                    pe.wait_ge(eq_ok, g + 1)
                    transposes(0, lambda t: eq[:, t, :]).then_inc(qT_ps, 1)
                    pe.wait_ge(vn_ok, g + 1)
                    transposes(1, lambda t: vn[:, 2 * t:2 * t + 2, :].rearrange("p a s -> p (a s)")).then_inc(vT_ps, 1)
                if cross_half:
                    pe.wait_ge(sx_ok, h + 1)
                    if not second:
                        pe.wait_ge(y2_ok, h)
                    for t in range(GT):
                        last = nc.tensor.matmul(bank[7][:, t * P:(t + 1) * P], sc_x[:, t, :], c_in[hp][:, t, :],
                                                start=True, stop=True)
                    last.then_inc(o2_ps, 1)
                if self_half:
                    pe.wait_ge(qT_ok, g + 1)
                    for t in range(GT):
                        last = nc.tensor.matmul(bank[2][:, t * P:(t + 1) * P],
                                                ek[:, 2 * t:2 * t + 2, :].rearrange("p a s -> p (a s)"),
                                                qT[:, t * P:(t + 1) * P], start=True, stop=True)
                    last.then_inc(sa_ps, 1)
                if cross_half:
                    pe.wait_ge(x2_ok, h + 1)
                    transposes(5, lambda t: x2[hp][:, t, :]).then_inc(x2T_ps, 1)
                if self_half:
                    pe.wait_ge(sa_ok, g + 1)
                    pe.wait_ge(v_ok, g + 1)
                    for t in range(GT):
                        last = nc.tensor.matmul(bank[3][:, t * P:(t + 1) * P], sc_a[:, t, :], v[:, t, :],
                                                start=True, stop=True)
                    last.then_inc(o1_ps, 1)
                if cross_half:
                    pe.wait_ge(x2T_ok, h + 1)
                    for t in range(GT):
                        last = nc.tensor.matmul(bank[4][:, t * E:(t + 1) * E], x2T[hp][:, t * P:(t + 1) * P],
                                                gwT[:, :], start=True, stop=True)
                    last.then_inc(l_ps, 1)

            steps(pe, step)

        @block.scalar
        def _(act):
            act.wait_ge(wT_ps, 1)
            nc.scalar.activation(wT[:, :, :].rearrange("p a d -> p (a d)"), bank[0][:, 0:3 * D], ACT.Copy)
            nc.scalar.activation(gwT[:, :], bank[0][:, 3 * D:3 * D + E], ACT.Copy).then_inc(wT_ok, 1)

            def step(i, j, par, first, second, self_half, cross_half):
                g, h, hj, hp = i, i - 1, (j if par else j - 1), 1 - par
                if self_half:
                    act.wait_ge(xT_ps, g + 1)
                    nc.scalar.activation(xT[:, :], bank[0][:, :], ACT.Copy).then_inc(xT_ok, 1)
                if cross_half:
                    act.wait_ge(cT_ps, h + 1)
                    nc.scalar.activation(cT[:, :], bank[4][:, :], ACT.Copy).then_inc(cT_ok, 1)
                    act.wait_ge(x1T_ps, h + 1)
                    nc.scalar.activation(x1T[:, :], bank[5][:, :], ACT.Copy).then_inc(x1T_ok, 1)
                if self_half:
                    act.wait_ge(q_ps, g + 1)
                    act.wait_ge(qmax_ok, g + 1)
                    for t in range(GT):
                        last = nc.scalar.activation(eq[:, t, :], tiles(1)[:, t, :], ACT.Exp, bias=nmax[:, t:t + 1],
                                                    accum_out=sums[:, t:t + 1])
                    last.then_inc(eq_ok, 1)
                    act.wait_ge(kvbias_ok, g + 1)
                    for n, e in enumerate((ek, ev)):
                        for b in range(GB):
                            at = GT + n * GB + b
                            last = nc.scalar.activation(e[:, b, :], batches(2 + n)[:, b, :], ACT.Exp,
                                                        bias=kvbias[:, n, b:b + 1], accum_out=sums[:, at:at + 1])
                    last.then_inc(exps_ok, 1)
                    act.wait_ge(vT_ps, g + 1)
                    nc.scalar.activation(v[:, :, :].rearrange("p t d -> p (t d)"), bank[1][:, :],
                                         ACT.Copy).then_inc(v_ok, 1)
                if cross_half:
                    act.wait_ge(x2T_ps, h + 1)
                    if not second:
                        act.wait_ge(stored[par], 48 * j)
                    nc.scalar.activation(x2T[hp][:, :], bank[5][:, :], ACT.Copy).then_inc(x2T_ok, 1)

            steps(act, step)

        @block.vector
        def _(dve):
            st_turn = [Turns(dve, st_ok[n], f"n_st{n}", 3 - n) for n in range(2)]
            l_turn = Turns(dve, l_ps, "n_l", 2)
            vs_turn = Turns(dve, vs_ok, "n_vs", 2)

            def step(i, j, par, first, second, self_half, cross_half):
                g, h, hj, hp = i, i - 1, (j if par else j - 1), 1 - par
                before = 0 if first else (N_SELF if second else N_SELF + (N_SELF + N_CROSS) * h)
                c = Done(dve, dve_self, before)

                def stats(n, y):
                    for t in range(GT):
                        last = nc.vector.bn_stats(st[n][:, t, :], y[:, t, :])
                    last.then_inc(st_ok[n], 1)
                    st_turn[n].wait((h if n else g) + 1)
                    for t in range(GT):
                        c.add(nc.vector.bn_aggr(mv[n][:, t, :], st[n][:, t, :]))
                    c.wait()

                def normalise(n, y, to):
                    for t in range(GT):
                        last = nc.vector.tensor_scalar(to[:, t, :], y[:, t, :], mv[n][:, t, 0:1], rs[n][:, t:t + 1],
                                                       ALU.subtract, ALU.mult)
                    return last

                if self_half:
                    dve.wait_ge(q_ps, g + 1)
                    nc.vector.reduce_max(nmax[:, :], tiles(1), AX.X, negate=True).then_inc(qmax_ok, 1)
                    dve.wait_ge(k_ps, g + 1)
                    c.add(nc.vector.reduce_max(kvmax[:, 0, :], batches(2), AX.X))
                    dve.wait_ge(v_ps, g + 1)
                    c.add(nc.vector.reduce_max(kvmax[:, 1, :], batches(3), AX.X))
                    c.wait()
                    for n in range(2):
                        c.add(nc.vector.tensor_scalar(kvneg[:, n, :], kvmax[:, n, :], bkv[:, n:n + 1], -1.0,
                                                      ALU.add, ALU.mult))
                    c.wait()
                    for n in range(2):
                        last = nc.vector.tensor_scalar(kvbias[:, n, :], kvneg[:, n, :], bkv[:, n:n + 1], None, ALU.add)
                    last.then_inc(kvbias_ok, 1)
                if cross_half:
                    dve.wait_ge(sx_ps, h + 1)
                    nc.vector.tensor_tensor(sc_x[:, :, :], tiles(6), across(mask_x[:, :], GT),
                                            ALU.mult).then_inc(sx_ok, 1)
                if self_half:
                    dve.wait_ge(exps_ok, g + 1)
                    nc.vector.reciprocal(rsum[:, :], sums[:, :]).then_inc(rsum_ok, 1)
                    dve.wait_ge(rsum_ok, g + 1)
                    dve.wait_ge(qT_ps, g + 1)
                    nc.vector.tensor_tensor(qT[:, :].rearrange("p (b s) -> p b s", b=GB), batches(0),
                                            over(rsum[:, GT:GT + GB], S), ALU.mult).then_inc(qT_ok, 1)
                if cross_half:
                    dve.wait_ge(o2_ps, h + 1)
                    nc.vector.tensor_tensor(y2[:, :, :], tiles(7), x1[hp][:, :, :], ALU.add).then_inc(y2_ok, 1)
                    dve.wait_ge(y2_ok, h + 1)
                    stats(1, y2)
                    nc.vector.tensor_scalar(ve[1][:, :], mv[1][:, :, 1], EPS, None, ALU.add).then_inc(ve2_ok, 1)
                if self_half:
                    dve.wait_ge(sa_ps, g + 1)
                    nc.vector.tensor_tensor(sc_a[:, :, :], tiles(2), across(mask_a[:, :], GT),
                                            ALU.mult).then_inc(sa_ok, 1)
                if cross_half:
                    dve.wait_ge(rs2_ok, h + 1)
                    if not second:
                        dve.wait_ge(stored[par], 48 * j)
                    normalise(1, y2, x2[hp]).then_inc(x2_ok, 1)
                if self_half:
                    dve.wait_ge(o1_ps, g + 1)
                    for t in range(GT):
                        last = nc.vector.scalar_tensor_tensor(y1[:, t, :], tiles(3)[:, t, :], rsum[:, t:t + 1],
                                                              x_in[par][:, t, :], ALU.mult, ALU.add)
                    last.then_inc(y1_ok, 1)
                    dve.wait_ge(y1_ok, g + 1)
                    stats(0, y1)
                    nc.vector.tensor_scalar(ve[0][:, :], mv[0][:, :, 1], EPS, None, ALU.add).then_inc(ve1_ok, 1)
                if cross_half:
                    l_turn.wait(h + 1)
                    for t in range(GT):
                        last = nc.vector.max(vs[:, t, :], bank[4][:, t * E:(t + 1) * E])
                    last.then_inc(vs_ok, 1)
                    vs_turn.wait(h + 1)
                    for t in range(GT):
                        c.add(nc.vector.max_index(ix[:, t, :], vs[:, t, :], bank[4][:, t * E:(t + 1) * E]))
                    c.wait()
                    nc.vector.tensor_copy(top_v[:, ds(h * GT, GT), :], vs[:, :, :])
                    nc.vector.tensor_copy(top_i[:, ds(h * GT, GT), :], ix[:, :, 0:K]).then_inc(top_ok, 1)
                if self_half:
                    dve.wait_ge(rs1_ok, g + 1)
                    normalise(0, y1, x1[par]).then_inc(x1_ok, 1)
                assert c.n == N_SELF * self_half + N_CROSS * cross_half

            steps(dve, step)


N_CONSTS = 10
N_SELF = 4 + GT
N_CROSS = 2 * GT


def routing(nc, sem, bank, m):
    w1, w3, w2, x2_all, x2T_all = m["w1"], m["w3"], m["w2"], m["x2_all"], m["x2T_all"]
    top_v, top_i, gates = m["top_v"], m["top_i"], m["gates"]
    src_tab, dst_tab, w_at = m["src_tab"], m["dst_tab"], m["w_at"]
    stack = ExitStack()
    with stack:
        def sb(name, shape, dt=F32):
            return stack.enter_context(nc.sbuf_tensor(name, shape, dt))

        NK = NT * K
        OH = GT * K
        iota_e = sb("iota_e", [P, E])
        before_m = sb("before_m", [P, P], BF16)
        ones_bf = sb("ones_bf", [P, P], BF16)
        ones_f = sb("ones_f", [P, NT])
        iota_row = sb("iota_row", [P, P], BF16)
        iota_blk = sb("iota_blk", [P, NB], BF16)
        first_slot = sb("first_slot", [P, NB])
        unused_row = sb("unused_row", [P, NB])
        tile_no = sb("tile_no", [P, NT])
        row_code = sb("row_code", [P, K])
        e8 = sb("e8", [P, NT, 8])
        ex8 = sb("ex8", [P, NT, 8])
        den = sb("den", [P, NT])
        rden = sb("rden", [P, NT])
        pick = [sb(f"pick{k}", [P, NT, E]) for k in range(K)]
        both = sb("both", [P, NT, E], BF16)
        cnt = sb("cnt", [P, E])
        cnt_i = [sb(f"cnt_i{n}", [P, E], I32) for n in range(2)]
        padded = sb("padded", [P, E])
        end = sb("end", [P, E])
        start = sb("start", [P, E])
        upto = sb("upto", [P, NT, E])
        pos = [sb(f"pos{n}", [P, NT, E]) for n in range(2)]
        hit = sb("hit", [P, NT, E])
        slot = sb("slot", [P, NT, K])
        slot_i = sb("slot_i", [P, NK], I32)
        slot_b = sb("slot_b", [P, NK], I32)
        slot_r = sb("slot_r", [P, NK], I32)
        blk = sb("blk", [P, NK])
        row = sb("row", [P, NK])
        own = [sb(f"own{n}", [P, NB]) for n in range(2)]
        oh_row = [sb(f"oh_row{n}", [P, P], BF16) for n in range(4)]
        oh_blk = [sb(f"oh_blk{n}", [P, 2, NB], BF16) for n in range(4)]
        sg = [sb(f"sg{n}", [P, GN]) for n in range(2)]
        hT = [sb(f"hT{n}", [P, FC, GN]) for n in range(2)]
        tab = [sb(f"tab{n}", [P, NB]) for n in range(5)]

        consts = sem("r_consts")
        exp_in = sem("r_exp_in")
        exp_ok = sem("r_exp_ok")
        both_ok = sem("r_both_ok")
        ranks_ps = sem("r_ranks_ps")
        pos_ok = sem("r_pos_ok")
        oh_ok = sem("r_oh_ok")
        oh_used = sem("r_oh_used")
        g_ps = sem("r_g_ps")
        u_ps = sem("r_u_ps")
        sg_ok = sem("r_sg_ok")
        hT_ok = sem("r_hT_ok")
        o_ps = sem("r_o_ps")
        added = sem("r_added")
        dve_self = sem("r_dve_self")

        def table(ap):
            return ap[:, :].rearrange("p (t e) -> p t e", e=E)

        block = stack.enter_context(nc.Block())

        def groups(engine, step):
            for g in range(2):
                step(g, 0, g, True)
            with engine.Fori(1, NG // 2) as j:
                for par in range(2):
                    step(j * 2 + par, j, par, False)

        @block.gpsimd
        def _(pool):
            c = Done(pool, consts)

            def iota(to, pattern, base, each):
                c.add(nc.gpsimd.iota(to, pattern, base=base, channel_multiplier=each,
                                     allow_small_or_imprecise_dtypes=True))

            c.add(nc.gpsimd.memset(before_m[:, :], 1.0))
            c.add(nc.gpsimd.memset(ones_bf[:, :], 1.0))
            c.add(nc.gpsimd.memset(ones_f[:, :], 1.0))
            c.wait()
            c.add(nc.gpsimd.affine_select(out=before_m[:, :], in_=before_m[:, :], compare_op=ALU.is_gt, fill=0.0,
                                          base=0, pattern=[[1, P]], channel_multiplier=-1))
            iota(iota_e[:, :], [[1, E]], 0, 0)
            iota(iota_row[:, :], [[1, P]], 0, 0)
            iota(iota_blk[:, :], [[1, NB]], 0, 0)
            iota(first_slot[:, :], [[P, NB]], 0, 0)
            iota(unused_row[:, :], [[P, NB]], T * K + 1, 1)
            iota(tile_no[:, :], [[1, NT]], 0, 0)
            iota(row_code[:, :], [[1, K]], 1, K)
            assert c.n == R_CONSTS

        @block.tensor
        def _(pe):
            pe.wait_ge(consts, R_CONSTS)
            pe.wait_ge(both_ok, 1)
            flat = both[:, :, :].rearrange("p t e -> p (t e)")
            nc.tensor.matmul(bank[0][:, :], before_m[:, :], flat, start=True, stop=True)
            nc.tensor.matmul(bank[1][:, :], ones_bf[:, :], flat, start=True, stop=True).then_inc(ranks_ps, 1)
            pe.wait_ge(pos_ok, 1)

            def rows(g, par, first):
                pe.wait_ge(hT_ok, (g + 1) * FC)
                if not first:
                    pe.wait_ge(added, g)
                for t in range(GT):
                    for c in range(FC):
                        last = nc.tensor.matmul(bank[4 + par][:, t * P:(t + 1) * P], hT[par][:, c, t * P:(t + 1) * P],
                                                w2[:, SHARED, c * D:(c + 1) * D], start=(c == 0), stop=(c == FC - 1))
                last.then_inc(o_ps, 1)

            def step(g, j, par, first):
                for c in range(FC):
                    n = g * FC + c
                    for ps, done, w, b, used in ((g_ps, sg_ok, w1, 0, sg_ok), (u_ps, hT_ok, w3, 2, hT_ok)):
                        if not (first and par == 0 and c < 2):
                            pe.wait_ge(used, n - 1)
                        nc.tensor.matmul(bank[b + c % 2][:, :], w[:, SHARED, c * P:(c + 1) * P],
                                         x2T_all[:, ds(g * GN, GN)], start=True, stop=True).then_inc(ps, 1)
                    if c == 1 and not (first and par == 0):
                        rows(g - 1, 1 - par, first)
                for q in range(OH):
                    pe.wait_ge(oh_ok, g * OH + q + 1)
                    start = first and par == 0 and q == 0
                    nc.tensor.matmul(bank[6][:, 0:2 * NB], oh_row[q % 4][:, :],
                                     oh_blk[q % 4][:, :, :].rearrange("p a n -> p (a n)"),
                                     start=start, stop=True, skip_group_check=True).then_inc(oh_used, 1)

            groups(pe, step)
            rows(NG - 1, 1, False)

        @block.scalar
        def _(act):
            act.wait_ge(exp_in, 1)
            nc.scalar.activation(ex8[:, :, :], e8[:, :, :], ACT.Exp).then_inc(exp_ok, 1)

            def step(g, j, par, first):
                for c in range(FC):
                    n = g * FC + c
                    act.wait_ge(g_ps, n + 1)
                    if not (first and par == 0 and c < 2):
                        act.wait_ge(hT_ok, n - 1)
                    nc.scalar.activation(sg[c % 2][:, :], bank[c % 2][:, :], ACT.Silu).then_inc(sg_ok, 1)

            groups(act, step)

        @block.vector
        def _(dve):
            c = Done(dve, dve_self)
            dve.wait_ge(consts, R_CONSTS)
            for k in range(K):
                c.add(nc.vector.tensor_tensor(pick[k][:, :, :], across(iota_e[:, :], NT), over(top_i[:, :, k], E),
                                              ALU.is_equal))
            c.wait()
            nc.vector.tensor_tensor(both[:, :, :], pick[0][:, :, :], pick[1][:, :, :], ALU.add).then_inc(both_ok, 1)
            nc.vector.tensor_tensor(e8[:, :, :], top_v[:, :, :], over(top_v[:, :, 0], 8),
                                    ALU.subtract).then_inc(exp_in, 1)
            dve.wait_ge(ranks_ps, 1)
            c.link(nc.vector.reduce_sum(cnt[:, :], table(bank[1]).rearrange("p t e -> p e t"), AX.X))
            c.link(nc.vector.tensor_scalar(cnt_i[0][:, :], cnt[:, :], float(P - 1), None, ALU.add))
            shift = P.bit_length() - 1
            c.link(nc.vector.tensor_scalar(cnt_i[1][:, :], cnt_i[0][:, :], shift, shift,
                                           ALU.logical_shift_right, ALU.logical_shift_left))
            c.link(nc.vector.tensor_copy(padded[:, :], cnt_i[1][:, :]))
            c.link(nc.vector.tensor_tensor_scan(end[:, :], ones_f[:, 0:E], padded[:, :], 0.0, ALU.mult, ALU.add))
            c.link(nc.vector.tensor_tensor(start[:, :], end[:, :], padded[:, :], ALU.subtract))
            for e in range(E):
                c.add(nc.vector.tensor_tensor_scan(upto[:, :, e], ones_f[:, :], table(bank[1])[:, :, e],
                                                   start[:, e:e + 1], ALU.mult, ALU.add))
            c.wait()
            c.link(nc.vector.tensor_tensor(pos[0][:, :, :], table(bank[1]), upto[:, :, :], ALU.subtract))
            nc.vector.tensor_tensor(pos[1][:, :, :], table(bank[0]), pos[0][:, :, :],
                                    ALU.subtract).then_inc(pos_ok, 1)
            dve.wait_ge(pos_ok, 1)
            for k in range(K):
                c.link(nc.vector.tensor_tensor(hit[:, :, :], pick[k][:, :, :], pos[1][:, :, :], ALU.mult))
                c.link(nc.vector.reduce_sum(slot[:, :, k], hit[:, :, :], AX.X))
            c.link(nc.vector.tensor_copy(slot_i[:, :], slot[:, :, :].rearrange("p t k -> p (t k)")))
            c.add(nc.vector.tensor_scalar(slot_b[:, :], slot_i[:, :], shift, None, ALU.logical_shift_right))
            c.add(nc.vector.tensor_scalar(slot_r[:, :], slot_i[:, :], P - 1, None, ALU.bitwise_and))
            c.wait()
            c.add(nc.vector.tensor_copy(blk[:, :], slot_b[:, :]))
            c.add(nc.vector.tensor_copy(row[:, :], slot_r[:, :]))
            c.wait()
            assert c.n == R_SELF

            def one_hots(g, first):
                for q in range(OH):
                    n = g * OH + q
                    if not (first and q < 4):
                        dve.wait_ge(oh_used, n - 3)
                    nc.vector.tensor_scalar(oh_row[q % 4][:, :], iota_row[:, :], row[:, ds(n, 1)], None, ALU.is_equal)
                    nc.vector.tensor_scalar(oh_blk[q % 4][:, 0, :], iota_blk[:, :], blk[:, ds(n, 1)],
                                            row_code[:, q % K:q % K + 1], ALU.is_equal, ALU.mult)
                    nc.vector.tensor_scalar(oh_blk[q % 4][:, 1, :], iota_blk[:, :], blk[:, ds(n, 1)],
                                            tile_no[:, ds(g * GT + q // K, 1)], ALU.is_equal, ALU.mult
                                            ).then_inc(oh_ok, 1)

            def add(g, par):
                dve.wait_ge(o_ps, g + 1)
                at = x2_all[:, ds(g * GT, GT), :].rearrange("p t d -> p (t d)")
                nc.vector.scalar_tensor_tensor(at, bank[4 + par][:, :], ALPHA / NS, at, ALU.mult,
                                               ALU.add).then_inc(added, 1)

            def step(g, j, par, first):
                for c in range(FC):
                    n = g * FC + c
                    dve.wait_ge(sg_ok, n + 1)
                    dve.wait_ge(u_ps, n + 1)
                    nc.vector.tensor_tensor(hT[par][:, c, :], sg[c % 2][:, :], bank[2 + c % 2][:, :],
                                            ALU.mult).then_inc(hT_ok, 1)
                    if c == 2 and not (first and par == 0):
                        add(g - 1, 1 - par)
                one_hots(g, first and par == 0)

            groups(dve, step)
            add(NG - 1, 1)
            dve.wait_ge(exp_ok, 1)
            c.link(nc.vector.reduce_sum(den[:, :], ex8[:, :, :], AX.X))
            c.link(nc.vector.reciprocal(rden[:, :], den[:, :]))
            for k in range(K):
                c.add(nc.vector.scalar_tensor_tensor(gates[:, k, :], rden[:, :], 1.0 - ALPHA, ex8[:, :, k],
                                                     ALU.mult, ALU.mult))
            c.add(nc.vector.memset(own[0][:, :], 0.0))
            c.wait()
            for e in range(E - 1):
                c.link(nc.vector.scalar_tensor_tensor(own[(e + 1) % 2][:, :], first_slot[:, :], end[:, e:e + 1],
                                                      own[e % 2][:, :], ALU.is_ge, ALU.add))
            c.add(nc.vector.tensor_scalar(w_at[:, :], own[(E - 1) % 2][:, :], float(F), None, ALU.mult))
            code, empty, less, moved, src = tab
            dve.wait_ge(oh_used, NK)
            c.link(nc.vector.tensor_scalar(code[:, :], bank[6][:, NB:2 * NB], float(K * P), None, ALU.mult))
            c.link(nc.vector.tensor_tensor(less[:, :], bank[6][:, 0:NB], code[:, :], ALU.add))
            c.add(nc.vector.tensor_scalar(empty[:, :], less[:, :], 0.0, None, ALU.is_equal))
            c.add(nc.vector.tensor_scalar(src[:, :], less[:, :], 1.0, 0.0, ALU.subtract, ALU.max))
            c.wait()
            c.link(nc.vector.tensor_tensor(moved[:, :], empty[:, :], unused_row[:, :], ALU.mult))
            c.link(nc.vector.scalar_tensor_tensor(code[:, :], less[:, :], -1.0, moved[:, :], ALU.add, ALU.add))
            c.add(nc.vector.tensor_copy(dst_tab[:, :], code[:, :]))
            c.link(nc.vector.tensor_copy(src_tab[:, :], src[:, :]))
            c.link(nc.vector.tensor_scalar(src_tab[:, :], src_tab[:, :], K.bit_length() - 1, None,
                                           ALU.logical_shift_right))


R_CONSTS = 11
R_SELF = 2 + 6 + E + 1 + 2 * K + 1 + 4


def experts(nc, sem, bank, m):
    w1, w3, w2, ident = m["w1"], m["w3"], m["w2"], m["ident"]
    src_tab, dst_tab, w_at = m["src_tab"], m["dst_tab"], m["w_at"]
    x2_rows, y_rows = m["x2_rows"], m["y_rows"]
    stack = ExitStack()
    with stack:
        def sb(name, shape, dt=F32):
            return stack.enter_context(nc.sbuf_tensor(name, shape, dt))

        src = [sb(f"src{n}", [P, 1], U32) for n in range(2)]
        dst = [sb(f"dst{n}", [P, 1], U32) for n in range(2)]
        xg = [sb(f"xg{n}", [P, D]) for n in range(2)]
        xT = [sb(f"e_xT{n}", [P, P]) for n in range(2)]
        sg = [sb(f"e_sg{n}", [P, F]) for n in range(2)]
        h = [sb(f"e_h{n}", [P, F]) for n in range(2)]
        hT = [sb(f"e_hT{n}", [P, F]) for n in range(2)]
        y = [sb(f"e_y{n}", [P, D]) for n in range(2)]

        src_ok = sem("e_src_ok")
        gathered = [sem(f"e_gathered{n}") for n in range(2)]
        scattered = [sem(f"e_scattered{n}") for n in range(2)]
        xT_ps = sem("e_xT_ps")
        xT_ok = sem("e_xT_ok")
        g_ps = sem("e_g_ps")
        u_ps = sem("e_u_ps")
        sg_ok = sem("e_sg_ok")
        h_ok = sem("e_h_ok")
        hT_ps = sem("e_hT_ps")
        hT_ok = sem("e_hT_ok")
        y_ps = sem("e_y_ps")
        y_ok = sem("e_y_ok")

        block = stack.enter_context(nc.Block())

        def steps(engine, step):
            for b in range(4):
                step(b, b // 2, b % 2)
            with engine.Fori(2, NB // 2 - 2) as j:
                for par in range(2):
                    step(j * 2 + par, j, par, inner=True)
            for b in range(NB - 4, NB + 1):
                step(b, b // 2, b % 2)

        @block.gpsimd
        def _(pool):
            src_turn = Turns(pool, src_ok, "n_src", 4 + 3 + 1)
            y_turn = Turns(pool, y_ok, "n_y", 3 + 1)

            def gather(b, par):
                src_turn.wait(b + 1)
                nc.gpsimd.indirect_dma_start(xg[par][:, :], None, x2_rows,
                                             bass.IndirectOffsetOnAxis(src[par][:, 0:1], 0)
                                             ).then_inc(gathered[par], 16)

            def scatter(b, par):
                y_turn.wait(b + 1)
                nc.gpsimd.indirect_dma_start(y_rows, bass.IndirectOffsetOnAxis(dst[par][:, 0:1], 0),
                                             y[par][:, :], None).then_inc(scattered[par], 16)

            for b in range(3):
                gather(b, b % 2)

            def step(b, j, par, inner=False):
                if inner or b + 3 < NB:
                    gather(b + 3, 1 - par)
                if inner or b >= 1:
                    scatter(b - 1, 1 - par)

            steps(pool, step)
            for n in range(2):
                pool.wait_ge(scattered[n], 16 * (NB // 2))

        @block.tensor
        def _(pe):
            def transposes_x(par, gathers):
                pe.wait_ge(gathered[par], 16 * gathers)
                nc.tensor.transpose(bank[7][:, 0:P], xg[par][:, :], ident[:, :]).then_inc(xT_ps, 1)

            transposes_x(0, 1)

            def step(b, j, par, inner=False):
                other = 1 - par
                if inner or b + 1 < NB:
                    pe.wait_ge(xT_ok, b + 1)
                    transposes_x(other, j + 1 + par)
                here = inner or b < NB
                if here:
                    at = pe.value_load(w_at[0:1, ds(b, 1)], min_val=0, max_val=(E - 1) * F)
                    pe.wait_ge(xT_ok, b + 1)
                    if inner or b >= 2:
                        pe.wait_ge(sg_ok, b - 1)
                    nc.tensor.matmul(bank[par][:, :], xT[par][:, :],
                                     w1[:, :, :].rearrange("p e f -> p (e f)")[:, ds(at, F)],
                                     start=True, stop=True).then_inc(g_ps, 1)
                if inner or b >= 1:
                    pe.wait_ge(h_ok, b)
                    if inner or b >= 3:
                        pe.wait_ge(hT_ok, b - 2)
                    for c in range(FC):
                        last = nc.tensor.transpose(bank[4 + other][:, c * P:(c + 1) * P],
                                                   h[other][:, c * P:(c + 1) * P], ident[:, :])
                    last.then_inc(hT_ps, 1)
                if here:
                    if inner or b >= 2:
                        pe.wait_ge(h_ok, b - 1)
                    nc.tensor.matmul(bank[2 + par][:, :], xT[par][:, :],
                                     w3[:, :, :].rearrange("p e f -> p (e f)")[:, ds(at, F)],
                                     start=True, stop=True).then_inc(u_ps, 1)
                if inner or b >= 1:
                    before = pe.value_load(w_at[0:1, ds(b - 1, 1)], min_val=0, max_val=(E - 1) * F)
                    pe.wait_ge(hT_ok, b)
                    if inner or b >= 2:
                        pe.wait_ge(y_ok, b - 1)
                    for c in range(FC):
                        last = nc.tensor.matmul(bank[6][:, 0:D], hT[other][:, c * P:(c + 1) * P],
                                                w2[:, :, :].rearrange("p e f -> p (e f)")[:, ds(before + c * D, D)],
                                                start=(c == 0), stop=(c == FC - 1))
                    last.then_inc(y_ps, 1)

            steps(pe, step)

        @block.scalar
        def _(act):
            def step(b, j, par, inner=False):
                other = 1 - par
                if inner or b >= 1:
                    act.wait_ge(hT_ps, b)
                    nc.scalar.activation(hT[other][:, :], bank[4 + other][:, :], ACT.Copy).then_inc(hT_ok, 1)
                if inner or b < NB:
                    act.wait_ge(g_ps, b + 1)
                    if inner or b >= 2:
                        act.wait_ge(h_ok, b - 1)
                    nc.scalar.activation(sg[par][:, :], bank[par][:, :], ACT.Silu).then_inc(sg_ok, 1)

            steps(act, step)

        @block.vector
        def _(dve):
            def stage(b, par):
                nc.vector.tensor_copy(src[par][:, :], src_tab[:, ds(b, 1)]).then_inc(src_ok, 1)

            def take_x(b, par):
                dve.wait_ge(xT_ps, b + 1)
                nc.vector.tensor_copy(xT[par][:, :], bank[7][:, 0:P]).then_inc(xT_ok, 1)

            stage(0, 0)
            stage(1, 1)
            take_x(0, 0)
            stage(2, 0)

            def step(b, j, par, inner=False):
                other = 1 - par
                if inner or b + 1 < NB:
                    take_x(b + 1, other)
                if inner or b + 3 < NB:
                    stage(b + 3, other)
                if inner or b >= 1:
                    dve.wait_ge(y_ps, b)
                    if inner or b >= 3:
                        dve.wait_ge(scattered[other], 16 * (j if par else j - 1))
                    nc.vector.tensor_copy(dst[other][:, :], dst_tab[:, ds(b - 1, 1)])
                    nc.vector.tensor_copy(y[other][:, :], bank[6][:, 0:D]).then_inc(y_ok, 1)
                if inner or b < NB:
                    dve.wait_ge(sg_ok, b + 1)
                    dve.wait_ge(u_ps, b + 1)
                    nc.vector.tensor_tensor(h[par][:, :], sg[par][:, :], bank[2 + par][:, :],
                                            ALU.mult).then_inc(h_ok, 1)

            steps(dve, step)


def combine(nc, sem, bank, m):
    x2_all, gates, minus_half, y_rows, out_rows = m["x2_all"], m["gates"], m["minus_half"], m["y_rows"], m["out_rows"]
    group_rows = m["group_rows"]
    stack = ExitStack()
    with stack:
        def sb(name, shape, dt=F32):
            return stack.enter_context(nc.sbuf_tensor(name, shape, dt))

        yk = [sb(f"yk{n}", [P, GT, K, D]) for n in range(2)]
        part = sb("part", [P, GT, D])
        z = [sb(f"z{n}", [P, GT, D]) for n in range(2)]
        res = [sb(f"res{n}", [P, GT, D]) for n in range(2)]
        st = sb("f_st", [P, GT, 6])
        mv = [sb(f"f_mv{n}", [P, GT, 2]) for n in range(2)]
        ve = [sb(f"f_ve{n}", [P, GT]) for n in range(2)]
        rs = [sb(f"f_rs{n}", [P, GT]) for n in range(2)]

        y_ld = [sem(f"f_y_ld{n}") for n in range(2)]
        stored = [sem(f"f_stored{n}") for n in range(2)]
        z_ok = sem("f_z_ok")
        ve_ok = sem("f_ve_ok")
        rs_ok = sem("f_rs_ok")
        res_ok = sem("f_res_ok")
        st_ok = sem("f_st_ok")
        dve_self = sem("f_dve_self")

        block = stack.enter_context(nc.Block())
        both = y_rows[0:T * K, :].rearrange("(n k) d -> n (k d)", k=K)

        @block.sync
        def _(sp):
            def load(g, par):
                sp.dma_start(yk[par][:, :, :, :].rearrange("p t k d -> p t (k d)"),
                             both[ds(g * GN, GN), :].rearrange("(t p) d -> p t d", p=P)).then_inc(y_ld[par], 16)

            for g in range(2):
                load(g, g)
            with sp.Fori(1, NG // 2) as j:
                for par in range(2):
                    g = j * 2 + par
                    sp.wait_ge(z_ok, g - 1)
                    load(g, par)

        @block.gpsimd
        def _(pool):
            with pool.Fori(0, NG // 2) as j:
                for par in range(2):
                    pool.wait_ge(ve_ok, j * 2 + par + 1)
                    nc.gpsimd.tensor_tensor(rs[par][:, :], ve[par][:, :], minus_half[:, 0:GT],
                                            ALU.pow).then_inc(rs_ok, 1)

        @block.vector
        def _(dve):
            st_turn = Turns(dve, st_ok, "n_f_st", 4)

            def sums(g, j, par, before):
                c = Done(dve, dve_self, before)
                dve.wait_ge(y_ld[par], 16 * (j + 1))
                for t in range(GT):
                    c.add(nc.vector.scalar_tensor_tensor(part[:, t, :], yk[par][:, t, 0, :],
                                                         gates[:, 0, ds(g * GT + t, 1)],
                                                         x2_all[:, ds(g * GT + t, 1), :].rearrange("p a d -> p (a d)"),
                                                         ALU.mult, ALU.add))
                c.wait()
                for t in range(GT):
                    last = nc.vector.scalar_tensor_tensor(z[par][:, t, :], yk[par][:, t, 1, :],
                                                          gates[:, 1, ds(g * GT + t, 1)], part[:, t, :],
                                                          ALU.mult, ALU.add)
                last.then_inc(z_ok, 1)
                dve.wait_ge(z_ok, g + 1)
                for t in range(GT):
                    last = nc.vector.bn_stats(st[:, t, :], z[par][:, t, :])
                last.then_inc(st_ok, 1)
                st_turn.wait(g + 1)
                for t in range(GT):
                    c.add(nc.vector.bn_aggr(mv[par][:, t, :], st[:, t, :]))
                c.wait()
                nc.vector.tensor_scalar(ve[par][:, :], mv[par][:, :, 1], EPS, None, ALU.add).then_inc(ve_ok, 1)
                assert c.n == N_SUMS

            def normalise(g, j, par, early):
                dve.wait_ge(rs_ok, g + 1)
                if not early:
                    dve.wait_ge(stored[par], 16 * j)
                for t in range(GT):
                    last = nc.vector.tensor_scalar(res[par][:, t, :], z[par][:, t, :], mv[par][:, t, 0:1],
                                                   rs[par][:, t:t + 1], ALU.subtract, ALU.mult)
                last.then_inc(res_ok, 1)

            sums(0, 0, 0, 0)
            sums(1, 0, 1, N_SUMS)
            normalise(0, 0, 0, True)
            sums(2, 1, 0, 2 * N_SUMS)
            normalise(1, 0, 1, True)
            with dve.Fori(1, NG // 2 - 1) as j:
                sums(j * 2 + 1, j, 1, (j * 2 + 1) * N_SUMS)
                normalise(j * 2, j, 0, False)
                sums(j * 2 + 2, j + 1, 0, (j * 2 + 2) * N_SUMS)
                normalise(j * 2 + 1, j, 1, False)
            j = NG // 2 - 1
            sums(NG - 1, j, 1, (NG - 1) * N_SUMS)
            normalise(NG - 2, j, 0, False)
            normalise(NG - 1, j, 1, False)

        @block.scalar
        def _(act):
            with act.Fori(0, NG // 2) as j:
                for par in range(2):
                    g = j * 2 + par
                    act.wait_ge(res_ok, g + 1)
                    act.dma_start(group_rows(out_rows, g), res[par][:, :, :]).then_inc(stored[par], 16)
            for n in range(2):
                act.wait_ge(stored[n], 16 * (NG // 2))


N_SUMS = 2 * GT

_INS = ["x", "ctx_1024", "L0_attn_Wq", "L0_attn_bq", "L0_attn_Wk", "L0_attn_bk", "L0_attn_Wv", "L0_attn_bv",
        "L0_ffn_gate_W", "L0_ffn_w1_e", "L0_ffn_w3_e", "L0_ffn_w2_e", "L0_ffn_w1_s", "L0_ffn_w3_s", "L0_ffn_w2_s"]


def kernel(**inputs):
    import numpy as _np
    import concourse.bacc as _bacc
    from concourse import mybir as _mybir
    from concourse.bass_utils import run_bass_kernel_spmd as _run

    nc = _bacc.Bacc("TRN2", target_bir_lowering=False, num_devices=1)
    arrays, args = {}, []
    for name in _INS:
        a = _np.ascontiguousarray(inputs[name])
        arrays[f"in_{name}_dram"] = a
        args.append(nc.dram_tensor(f"in_{name}_dram", a.shape, _mybir.dt.from_np(a.dtype), kind="ExternalInput").ap())
    out = nc.dram_tensor("out_0_dram", (B, S, D), _mybir.dt.float32, kind="ExternalOutput").ap()
    decoder(nc, *args, out)
    r = _run(nc, [arrays], core_ids=[0])
    return r.results[0]["out_0_dram"]
```

```python
from contextlib import ExitStack

import concourse.bass as bass
from concourse import mybir

F32 = mybir.dt.float32
BF16 = mybir.dt.bfloat16
I32 = mybir.dt.int32
U32 = mybir.dt.uint32
ACT = mybir.ActivationFunctionType
ALU = mybir.AluOpType
AX = mybir.AxisListType
ds = bass.ds

P = 128
B, S, D = 128, 64, 128
T = B * S
GT = 4
GN = GT * P
NG = T // GN
NT = T // P
GB = GN // S
E, F, K = 8, 512, 2
FC = F // P
NS, FS = 8, 64
SHARED = E
NB = T * K // P + E
EPS = 1e-5
Q_SCALE = float(D) ** -0.5
X_SCALE = 1.0 / S
ALPHA = 0.5
assert NS * FS == F and NB % 2 == 0 and NG % 2 == 0 and NT <= 256 and 2 * P <= 256 and NB <= 256


class Done:

    def __init__(self, engine, sem, before=0):
        self.engine, self.sem, self.before, self.n = engine, sem, before, 0

    def add(self, instruction):
        self.n += 1
        return instruction.then_inc(self.sem, 1)

    def wait(self):
        self.engine.wait_ge(self.sem, self.before + self.n)

    def link(self, instruction):
        self.add(instruction)
        self.wait()


class Turns:

    def __init__(self, engine, sem, name, first):
        self.engine, self.sem, self.count = engine, sem, engine.alloc_register(name)
        engine.reg_mov(self.count, first)

    def wait(self, value):
        if isinstance(value, int):
            self.engine.wait_ge(self.sem, value)
        else:
            self.engine.wait_ge(self.sem, self.engine.snap(self.count))
            self.engine.reg_add(self.count, self.count, 1)


def over(ap, n):
    return ap.unsqueeze(2).broadcast_to([ap.shape[0], ap.shape[1], n])


def across(ap, n):
    return ap.unsqueeze(1).broadcast_to([ap.shape[0], n, ap.shape[1]])


def decoder(nc, x, ctx, wq, bq, wk, bk, wv, bv, gate_w, w1_e, w3_e, w2_e, w1_s, w3_s, w2_s, out):
    stack = ExitStack()
    with stack:
        def sb(name, shape, dt=F32):
            return stack.enter_context(nc.sbuf_tensor(name, shape, dt))

        def sem(name):
            return stack.enter_context(nc.semaphore(name))

        bank = [stack.enter_context(nc.psum_tensor(f"bank{i}", [P, 512], F32)) for i in range(8)]

        x_rows = x.rearrange("b s d -> (b s) d")
        ctx_rows = ctx.rearrange("b s d -> (b s) d")
        out_rows = out.rearrange("b s d -> (b s) d")
        x2_rows = nc.dram_tensor("x2_rows", (T, D), F32, kind="Internal").ap()
        x2T_cols = nc.dram_tensor("x2T_cols", (D, T), F32, kind="Internal").ap()
        y_rows = nc.dram_tensor("y_rows", (T * K + NB * P, D), F32, kind="Internal").ap()

        def group_rows(rows, g):
            return rows[ds(g * GN, GN), :].rearrange("(j p) d -> p j d", p=P)

        w1 = sb("w1", [P, E + 1, F])
        w3 = sb("w3", [P, E + 1, F])
        w2 = sb("w2", [P, E + 1, FC * D])
        x2_all = sb("x2_all", [P, NT, D])
        ident = sb("ident", [P, P])
        top_v = sb("top_v", [P, NT, 8])
        top_i = sb("top_i", [P, NT, K])
        gates = sb("gates", [P, K, NT])
        src_tab = sb("src_tab", [P, NB], U32)
        dst_tab = sb("dst_tab", [P, NB], U32)
        w_at = sb("w_at", [P, NB], I32)
        minus_half = sb("minus_half", [P, 2 * GT])
        weights_in = sem("weights_in")

        attention(nc, sem, bank, locals())
        routing(nc, sem, bank, locals())
        experts(nc, sem, bank, locals())
        combine(nc, sem, bank, locals())


def attention(nc, sem, bank, m):
    bk, bv, bq, gate_w = m["bk"], m["bv"], m["bq"], m["gate_w"]
    group_rows, x_rows, ctx_rows = m["group_rows"], m["x_rows"], m["ctx_rows"]
    x2_rows, x2T_cols = m["x2_rows"], m["x2T_cols"]
    w1, w3, w2, ident = m["w1"], m["w3"], m["w2"], m["ident"]
    x2_all, top_v, top_i = m["x2_all"], m["top_v"], m["top_i"]
    minus_half, weights_in = m["minus_half"], m["weights_in"]
    stack = ExitStack()
    with stack:
        def sb(name, shape, dt=F32):
            return stack.enter_context(nc.sbuf_tensor(name, shape, dt))

        def pair(name, shape, dt=F32):
            return [sb(f"{name}{n}", shape, dt) for n in range(2)]

        def sems(names):
            return [sem(n) for n in names.split()]

        w_raw = sb("w_raw", [P, 3, D])
        gw_raw = sb("gw_raw", [E, D])
        wT = sb("wT", [P, 3, D])
        gwT = sb("gwT", [P, E])
        bq_row = sb("bq_row", [1, GT, D])
        ones_row = sb("ones_row", [1, P])
        bkv = sb("bkv", [P, 2])
        mask_a = sb("mask_a", [P, P])
        mask_x = sb("mask_x", [P, P])
        x_in = pair("x_in", [P, GT, D])
        x_res = pair("x_res", [P, GT, D])
        c_in = pair("c_in", [P, GT, D])
        xT = sb("xT", [P, GN])
        cT = sb("cT", [P, GN])
        x1T = sb("x1T", [P, GN])
        x2T = pair("x2T", [P, GN])
        eq = sb("eq", [P, GT, D])
        ek = pair("ek", [P, GB, S])
        ev = sb("ev", [P, GB, S])
        qT = pair("qT", [P, GN])
        vn = sb("vn", [P, GB, S])
        v = pair("v", [P, GT, D])
        sc_a = sb("sc_a", [P, GT, P])
        sc_x = sb("sc_x", [P, GT, P])
        y1 = sb("y1", [P, GT, D])
        y2 = sb("y2", [P, GT, D])
        x1 = pair("x1_", [P, GT, D])
        x2 = pair("x2_", [P, GT, D])
        nmax = sb("nmax", [P, GT])
        kvmax = sb("kvmax", [P, 2, GB])
        kvneg = sb("kvneg", [P, 2, GB])
        kvbias = sb("kvbias", [P, 2, GB])
        sums = pair("sums", [P, GT + 2 * GB])
        rsum = pair("rsum", [P, GT + 2 * GB])
        st = pair("st", [P, GT, 6])
        mv = pair("mv", [P, GT, 2])
        ve = pair("ve", [P, GT])
        rs = pair("rs", [P, GT])
        vs = sb("vs", [P, GT, 8])
        ix = sb("ix", [P, GT, 8], U32)

        small_in, consts, wT_ps, wT_ok = sems("small_in consts wT_ps wT_ok")
        x_ld, r_ld, c_ld, stored = (sems(f"{n}0 {n}1") for n in ("x_ld", "r_ld", "c_ld", "stored"))
        xT_ps, xT_ok, q_ps, k_ps, v_ps, qmax_ok, kvmax_ok, kvneg_ok, kvbias_ok = sems(
            "xT_ps xT_ok q_ps k_ps v_ps qmax_ok kvmax_ok kvneg_ok kvbias_ok")
        eq_ok, ek_ok, ev_ok, rsum_ok, vn_ok, qT_ps, qT_ok, vT_ps, v_ok = sems(
            "eq_ok ek_ok ev_ok rsum_ok vn_ok qT_ps qT_ok vT_ps v_ok")
        sa_ps, sa_ok, o1_ps, cT_ps, cT_ok, x1T_ps, x1T_ok, sx_ps, sx_ok, o2_ps = sems(
            "sa_ps sa_ok o1_ps cT_ps cT_ok x1T_ps x1T_ok sx_ps sx_ok o2_ps")
        y_ok, st_ok, mv_ok, ve_ok, rs_ok, xn_ok = (
            sems(f"{n}1 {n}2") for n in ("y_ok", "st_ok", "mv_ok", "ve_ok", "rs_ok", "xn_ok"))
        x2T_ps, x2T_ok, l_ps, vs_ok, ix_ok, top_ok = sems("x2T_ps x2T_ok l_ps vs_ok ix_ok top_ok")

        def tiles(b):
            return bank[b][:, :].rearrange("p (j n) -> p j n", j=GT)

        def batches(b):
            return bank[b][:, :].rearrange("p (j n) -> p j n", j=GB)

        def later(g, n):
            return not isinstance(g, int) or g >= n

        def steps(engine, step, first, stages):
            def at_of(j, par, known):
                def at(s):
                    if known is not None and not 0 <= known - s < NG:
                        return None
                    return (j * 2 + par - s, j + (par - s) // 2, (par - s) % 2)
                return at

            for i in range(first):
                step(at_of(i // 2, i % 2, i))
            with engine.Fori(first // 2, NG // 2) as j:
                for par in range(2):
                    step(at_of(j, par, None))
            for i in range(NG, NG + stages - 1):
                step(at_of(i // 2, i % 2, i))

        FIRST, STAGES = 6, 5
        PROJECT, SOFTEN, MIX, CROSS, ROUTE = range(STAGES)

        block = stack.enter_context(nc.Block())

        @block.sync
        def _(sp):
            for n, w in enumerate((m["wq"], m["wk"], m["wv"])):
                sp.dma_start(w_raw[:, n, :], w).then_inc(small_in, 16)
            sp.dma_start(gw_raw[:, :], gate_w).then_inc(small_in, 16)
            for j in range(GT):
                sp.dma_start(bq_row[:, j, :], bq.rearrange("(a n) -> a n", a=1)).then_inc(small_in, 16)
            sp.dma_start(bkv[:, 0:1], bk.rearrange("(n a) -> n a", a=1)).then_inc(small_in, 16)
            sp.dma_start(bkv[:, 1:2], bv.rearrange("(n a) -> n a", a=1)).then_inc(small_in, 16)

            def step(at):
                if now := at(0):
                    g, gj, gp = now
                    if later(g, 2):
                        sp.wait_ge(xT_ps, g - 1)
                    sp.dma_start(x_in[gp][:, :, :], group_rows(x_rows, g)).then_inc(x_ld[gp], 16)
                if now := at(6):
                    g, gj, gp = now
                    sp.wait_ge(x2T_ok, g + 1)
                    sp.dma_start(group_rows(x2_rows, g), x2[gp][:, :, :]).then_inc(stored[gp], 16)
                    sp.dma_start(x2_all[:, ds(g * GT, GT), :], x2[gp][:, :, :]).then_inc(stored[gp], 16)
                    sp.dma_start(x2T_cols[:, ds(g * GN, GN)], x2T[gp][:, :]).then_inc(stored[gp], 16)
                if now := at(2):
                    g, gj, gp = now
                    if later(g, 2):
                        sp.wait_ge(y_ok[0], g - 1)
                    sp.dma_start(x_res[gp][:, :, :], group_rows(x_rows, g)).then_inc(r_ld[gp], 16)
                if now := at(3):
                    g, gj, gp = now
                    if later(g, 2):
                        sp.wait_ge(o2_ps, g - 1)
                    sp.dma_start(c_in[gp][:, :, :], group_rows(ctx_rows, g)).then_inc(c_ld[gp], 16)

            steps(sp, step, FIRST, 7)
            for par in range(2):
                sp.wait_ge(stored[par], 48 * (NG // 2))

        @block.gpsimd
        def _(pool):
            c = Done(pool, consts)
            c.add(nc.gpsimd.memset(ident[:, :], 0.0))
            c.add(nc.gpsimd.memset(ones_row[:, :], 1.0))
            c.add(nc.gpsimd.memset(minus_half[:, :], -0.5))
            for mask, value in ((mask_a, Q_SCALE), (mask_x, X_SCALE)):
                c.add(nc.gpsimd.memset(mask[:, :], 0.0))
                c.wait()
                c.link(nc.gpsimd.memset(mask[0:S, 0:S], value))
                c.link(nc.gpsimd.memset(mask[S:P, S:P], value))
            c.wait()
            c.add(nc.gpsimd.affine_select(out=ident[:, :], in_=ident[:, :], compare_op=ALU.not_equal, fill=1.0,
                                          base=0, pattern=[[-1, P]], channel_multiplier=1))
            assert c.n == N_CONSTS
            def normalise(n, g, y, to):
                pool.wait_ge(ve_ok[n], g + 1)
                nc.gpsimd.tensor_tensor(rs[n][:, :], ve[n][:, :], minus_half[:, 0:GT], ALU.pow)
                nc.gpsimd.tensor_tensor(to[:, :, :], y[:, :, :], over(mv[n][:, :, 0], D),
                                        ALU.subtract).then_inc(rs_ok[n], 1)
                pool.wait_ge(rs_ok[n], g + 1)
                nc.gpsimd.tensor_tensor(to[:, :, :], to[:, :, :], over(rs[n][:, :], D),
                                        ALU.mult).then_inc(xn_ok[n], 1)

            def step(at):
                if now := at(MIX):
                    g, gj, gp = now
                    if later(g, 2):
                        pool.wait_ge(y_ok[1], g - 1)
                    normalise(0, g, y1, x1[gp])
                if now := at(SOFTEN):
                    g, gj, gp = now
                    pool.wait_ge(rsum_ok, g + 1)
                    nc.gpsimd.tensor_tensor(vn[:, :, :], ev[:, :, :], over(rsum[gp][:, GT + GB:], S),
                                            ALU.mult).then_inc(vn_ok, 1)
                if now := at(CROSS):
                    g, gj, gp = now
                    if later(g, 2):
                        pool.wait_ge(stored[gp], 48 * gj)
                    normalise(1, g, y2, x2[gp])

            steps(pool, step, FIRST, STAGES)

        @block.tensor
        def _(pe):
            pe.wait_ge(small_in, 16 * 10)
            pe.wait_ge(consts, N_CONSTS)
            for n in range(3):
                nc.tensor.transpose(bank[0][:, n * D:(n + 1) * D], w_raw[:, n, :], ident[:, :])
            nc.tensor.transpose(bank[0][:, 3 * D:3 * D + E], gw_raw[:, :], ident[0:E, 0:E]).then_inc(wT_ps, 1)
            pe.wait_ge(wT_ok, 1)

            def transposes(b, of):
                for t in range(GT):
                    last = nc.tensor.transpose(bank[b][:, t * P:(t + 1) * P], of(t), ident[:, :])
                return last

            def products(b, lhsT, rhs):
                for t in range(GT):
                    last = nc.tensor.matmul(bank[b][:, t * P:(t + 1) * P], lhsT(t), rhs(t), start=True, stop=True)
                return last

            def two(ap, t):
                return ap[:, 2 * t:2 * t + 2, :].rearrange("p a s -> p (a s)")

            def step(at):
                project, soften, mix, cross, route = (at(s) for s in range(STAGES))
                if mix:
                    g, gj, gp = mix
                    pe.wait_ge(qT_ok, g + 1)
                    if later(g, 1):
                        pe.wait_ge(y_ok[0], g)
                    products(4, lambda t: two(ek[gp], t), lambda t: qT[gp][:, t * P:(t + 1) * P]).then_inc(sa_ps, 1)
                if project:
                    g, gj, gp = project
                    pe.wait_ge(x_ld[gp], 16 * (gj + 1))
                    if soften and not mix:
                        pe.wait_ge(xT_ok, g)
                    transposes(0, lambda t: x_in[gp][:, t, :]).then_inc(xT_ps, 1)
                if cross:
                    g, gj, gp = cross
                    pe.wait_ge(c_ld[gp], 16 * (gj + 1))
                    if later(g, 1):
                        pe.wait_ge(sx_ok, g)
                    transposes(5, lambda t: c_in[gp][:, t, :]).then_inc(cT_ps, 1)
                    pe.wait_ge(xn_ok[0], g + 1)
                    if later(g, 1):
                        pe.wait_ge(y_ok[1], g)
                    transposes(6, lambda t: x1[gp][:, t, :]).then_inc(x1T_ps, 1)
                if project:
                    g, gj, gp = project
                    pe.wait_ge(xT_ok, g + 1)
                    if soften:
                        pe.wait_ge(eq_ok, g)
                    nc.tensor.matmul(bank[1][:, :], ones_row[:, :], bq_row[:, :, :].rearrange("a j d -> a (j d)"),
                                     start=True, stop=False)
                    for t in range(GT):
                        last = nc.tensor.matmul(bank[1][:, t * P:(t + 1) * P], xT[:, t * P:(t + 1) * P],
                                                wT[:, 0, :], start=False, stop=(t == GT - 1))
                    last.then_inc(q_ps, 1)
                if mix:
                    g, gj, gp = mix
                    pe.wait_ge(vn_ok, g + 1)
                    if project:
                        pe.wait_ge(xT_ok, g + 3)
                    transposes(0, lambda t: two(vn, t)).then_inc(vT_ps, 1)
                if mix:
                    g, gj, gp = mix
                    pe.wait_ge(v_ok, g + 1)
                    pe.wait_ge(sa_ok, g + 1)
                    products(4, lambda t: sc_a[:, t, :], lambda t: v[gp][:, t, :]).then_inc(o1_ps, 1)
                if cross:
                    g, gj, gp = cross
                    pe.wait_ge(cT_ok, g + 1)
                    pe.wait_ge(x1T_ok, g + 1)
                    products(5, lambda t: cT[:, t * P:(t + 1) * P],
                             lambda t: x1T[:, t * P:(t + 1) * P]).then_inc(sx_ps, 1)
                if soften:
                    g, gj, gp = soften
                    pe.wait_ge(eq_ok, g + 1)
                    if mix:
                        pe.wait_ge(v_ok, g)
                    transposes(0, lambda t: eq[:, t, :]).then_inc(qT_ps, 1)
                if route:
                    g, gj, gp = route
                    pe.wait_ge(xn_ok[1], g + 1)
                    if later(g, 1):
                        pe.wait_ge(top_ok, g)
                    transposes(7, lambda t: x2[gp][:, t, :]).then_inc(x2T_ps, 1)
                if project:
                    g, gj, gp = project
                    if later(g, 1):
                        pe.wait_ge(ek_ok, g)
                    nc.tensor.matmul(bank[2][:, :], wT[:, 1, :], xT[:, :], start=True, stop=True).then_inc(k_ps, 1)
                if cross:
                    g, gj, gp = cross
                    pe.wait_ge(sx_ok, g + 1)
                    products(6, lambda t: sc_x[:, t, :], lambda t: c_in[gp][:, t, :]).then_inc(o2_ps, 1)
                if project:
                    g, gj, gp = project
                    if later(g, 1):
                        pe.wait_ge(ev_ok, g)
                    nc.tensor.matmul(bank[3][:, :], wT[:, 2, :], xT[:, :], start=True, stop=True).then_inc(v_ps, 1)

                if route:
                    g, gj, gp = route
                    pe.wait_ge(x2T_ok, g + 1)
                    for t in range(GT):
                        last = nc.tensor.matmul(bank[7][:, t * E:(t + 1) * E], x2T[gp][:, t * P:(t + 1) * P],
                                                gwT[:, :], start=True, stop=True)
                    last.then_inc(l_ps, 1)

            steps(pe, step, FIRST, STAGES)

        @block.scalar
        def _(act):
            act.wait_ge(x_ld[1], 16)
            act.dma_start(w1[:, 0:E, :], m["w1_e"].rearrange("e d f -> d e f")).then_inc(weights_in, 16)
            act.dma_start(w3[:, 0:E, :], m["w3_e"].rearrange("e d f -> d e f")).then_inc(weights_in, 16)
            act.dma_start(w1[:, SHARED, :].rearrange("d (n f) -> d n f", n=NS),
                          m["w1_s"].rearrange("n d f -> d n f")).then_inc(weights_in, 16)
            act.dma_start(w3[:, SHARED, :].rearrange("d (n f) -> d n f", n=NS),
                          m["w3_s"].rearrange("n d f -> d n f")).then_inc(weights_in, 16)
            for e in range(E):
                act.dma_start(w2[:, e, :].rearrange("p (c d) -> p c d", c=FC),
                              m["w2_e"][e].rearrange("(c p) d -> p c d", p=P)).then_inc(weights_in, 16)
            act.dma_start(w2[:, SHARED, :].rearrange("p (c d) -> p c d", c=FC),
                          m["w2_s"].rearrange("n f d -> (n f) d").rearrange("(c p) d -> p c d", p=P)
                          ).then_inc(weights_in, 16)
            act.wait_ge(wT_ps, 1)
            nc.scalar.activation(wT[:, :, :].rearrange("p a d -> p (a d)"), bank[0][:, 0:3 * D], ACT.Copy)
            nc.scalar.activation(gwT[:, :], bank[0][:, 3 * D:3 * D + E], ACT.Copy).then_inc(wT_ok, 1)

            def exps(n, e, gp):
                for b in range(GB):
                    col = GT + n * GB + b
                    last = nc.scalar.activation(e[:, b, :], batches(2 + n)[:, b, :], ACT.Exp,
                                                bias=kvbias[:, n, b:b + 1], accum_out=sums[gp][:, col:col + 1])
                return last

            def step(at):
                project, soften, mix, cross, route = (at(s) for s in range(STAGES))
                if soften:
                    g, gj, gp = soften
                    act.wait_ge(qmax_ok, g + 1)
                    if later(g, 1):
                        act.wait_ge(qT_ps, g)
                    for t in range(GT):
                        last = nc.scalar.activation(eq[:, t, :], tiles(1)[:, t, :], ACT.Exp, bias=nmax[:, t:t + 1],
                                                    accum_out=sums[gp][:, t:t + 1])
                    last.then_inc(eq_ok, 1)
                if project:
                    g, gj, gp = project
                    act.wait_ge(xT_ps, g + 1)
                    nc.scalar.activation(xT[:, :], bank[0][:, :], ACT.Copy).then_inc(xT_ok, 1)
                if cross:
                    g, gj, gp = cross
                    act.wait_ge(cT_ps, g + 1)
                    nc.scalar.activation(cT[:, :], bank[5][:, :], ACT.Copy).then_inc(cT_ok, 1)
                    act.wait_ge(x1T_ps, g + 1)
                    nc.scalar.activation(x1T[:, :], bank[6][:, :], ACT.Copy).then_inc(x1T_ok, 1)
                if mix:
                    g, gj, gp = mix
                    act.wait_ge(vT_ps, g + 1)
                    nc.scalar.activation(v[gp][:, :, :].rearrange("p t d -> p (t d)"), bank[0][:, :],
                                         ACT.Copy).then_inc(v_ok, 1)
                if soften:
                    g, gj, gp = soften
                    act.wait_ge(kvbias_ok, g + 1)
                    exps(0, ek[gp], gp).then_inc(ek_ok, 1)
                    exps(1, ev, gp).then_inc(ev_ok, 1)
                if route:
                    g, gj, gp = route
                    act.wait_ge(x2T_ps, g + 1)
                    if later(g, 2):
                        act.wait_ge(stored[gp], 48 * gj)
                    nc.scalar.activation(x2T[gp][:, :], bank[7][:, :], ACT.Copy).then_inc(x2T_ok, 1)

            steps(act, step, FIRST, STAGES)
            act.wait_ge(weights_in, 16 * (5 + E))

        @block.vector
        def _(dve):
            st_turn = [Turns(dve, st_ok[n], f"n_st{n}", 5 - n) for n in range(2)]
            l_turn = Turns(dve, l_ps, "n_l", 3)
            vs_turn = Turns(dve, vs_ok, "n_vs", 3)

            def stats(n, g, y):
                dve.wait_ge(y_ok[n], g + 1)
                for t in range(GT):
                    last = nc.vector.bn_stats(st[n][:, t, :], y[:, t, :])
                last.then_inc(st_ok[n], 1)
                st_turn[n].wait(g + 1)
                for t in range(GT):
                    last = nc.vector.bn_aggr(mv[n][:, t, :], st[n][:, t, :])
                last.then_inc(mv_ok[n], 1)
                dve.wait_ge(mv_ok[n], g + 1)
                nc.vector.tensor_scalar(ve[n][:, :], mv[n][:, :, 1], EPS, None, ALU.add).then_inc(ve_ok[n], 1)

            def step(at):
                project, soften, mix, cross, route = (at(s) for s in range(STAGES))
                if mix:
                    g, gj, gp = mix
                    dve.wait_ge(sa_ps, g + 1)
                    nc.vector.tensor_tensor(sc_a[:, :, :], tiles(4), across(mask_a[:, :], GT),
                                            ALU.mult).then_inc(sa_ok, 1)
                if mix:
                    g, gj, gp = mix
                    dve.wait_ge(o1_ps, g + 1)
                    dve.wait_ge(r_ld[gp], 16 * (gj + 1))
                    if later(g, 1):
                        dve.wait_ge(xn_ok[0], g)
                    for t in range(GT):
                        last = nc.vector.scalar_tensor_tensor(y1[:, t, :], tiles(4)[:, t, :], rsum[gp][:, t:t + 1],
                                                              x_res[gp][:, t, :], ALU.mult, ALU.add)
                    last.then_inc(y_ok[0], 1)
                if cross:
                    g, gj, gp = cross
                    dve.wait_ge(sx_ps, g + 1)
                    nc.vector.tensor_tensor(sc_x[:, :, :], tiles(5), across(mask_x[:, :], GT),
                                            ALU.mult).then_inc(sx_ok, 1)
                if mix:
                    g, gj, gp = mix
                    stats(0, g, y1)
                if project:
                    g, gj, gp = project
                    dve.wait_ge(q_ps, g + 1)
                    nc.vector.reduce_max(nmax[:, :], tiles(1), AX.X, negate=True).then_inc(qmax_ok, 1)
                if soften:
                    g, gj, gp = soften
                    dve.wait_ge(ev_ok, g + 1)
                    nc.vector.reciprocal(rsum[gp][:, :], sums[gp][:, :]).then_inc(rsum_ok, 1)
                    dve.wait_ge(rsum_ok, g + 1)
                    dve.wait_ge(qT_ps, g + 1)
                    nc.vector.tensor_tensor(qT[gp][:, :].rearrange("p (b s) -> p b s", b=GB), batches(0),
                                            over(rsum[gp][:, GT:GT + GB], S), ALU.mult).then_inc(qT_ok, 1)
                if project:
                    g, gj, gp = project
                    dve.wait_ge(k_ps, g + 1)
                    nc.vector.reduce_max(kvmax[:, 0, :], batches(2), AX.X)
                if cross:
                    g, gj, gp = cross
                    dve.wait_ge(o2_ps, g + 1)
                    if later(g, 1):
                        dve.wait_ge(xn_ok[1], g)
                    nc.vector.tensor_tensor(y2[:, :, :], tiles(6), x1[gp][:, :, :], ALU.add).then_inc(y_ok[1], 1)
                    stats(1, g, y2)
                if project:
                    g, gj, gp = project
                    dve.wait_ge(v_ps, g + 1)
                    nc.vector.reduce_max(kvmax[:, 1, :], batches(3), AX.X).then_inc(kvmax_ok, 1)
                if route:
                    g, gj, gp = route
                    l_turn.wait(g + 1)
                    for t in range(GT):
                        last = nc.vector.max(vs[:, t, :], bank[7][:, t * E:(t + 1) * E])
                    last.then_inc(vs_ok, 1)
                if project:
                    g, gj, gp = project
                    dve.wait_ge(kvmax_ok, g + 1)
                    for n in range(2):
                        last = nc.vector.tensor_scalar(kvneg[:, n, :], kvmax[:, n, :], bkv[:, n:n + 1], -1.0,
                                                       ALU.add, ALU.mult)
                    last.then_inc(kvneg_ok, 1)
                if route:
                    g, gj, gp = route
                    vs_turn.wait(g + 1)
                    for t in range(GT):
                        last = nc.vector.max_index(ix[:, t, :], vs[:, t, :], bank[7][:, t * E:(t + 1) * E])
                    last.then_inc(ix_ok, 1)
                if project:
                    g, gj, gp = project
                    dve.wait_ge(kvneg_ok, g + 1)
                    for n in range(2):
                        last = nc.vector.tensor_scalar(kvbias[:, n, :], kvneg[:, n, :], bkv[:, n:n + 1], None, ALU.add)
                    last.then_inc(kvbias_ok, 1)
                if route:
                    g, gj, gp = route
                    dve.wait_ge(ix_ok, g + 1)
                    nc.vector.tensor_copy(top_v[:, ds(g * GT, GT), :], vs[:, :, :])
                    nc.vector.tensor_copy(top_i[:, ds(g * GT, GT), :], ix[:, :, 0:K]).then_inc(top_ok, 1)

            steps(dve, step, FIRST, STAGES)


N_CONSTS = 10


def routing(nc, sem, bank, m):
    w1, w3, w2, x2_all, x2T_cols = m["w1"], m["w3"], m["w2"], m["x2_all"], m["x2T_cols"]
    top_v, top_i, gates = m["top_v"], m["top_i"], m["gates"]
    src_tab, dst_tab, w_at = m["src_tab"], m["dst_tab"], m["w_at"]
    stack = ExitStack()
    with stack:
        def sb(name, shape, dt=F32):
            return stack.enter_context(nc.sbuf_tensor(name, shape, dt))

        NK = NT * K
        OH = GT * K
        OC = OH // FC
        iota_e = sb("iota_e", [P, E])
        before_m = sb("before_m", [P, P], BF16)
        ones_bf = sb("ones_bf", [P, P], BF16)
        ones_f = sb("ones_f", [P, NT])
        iota_row = sb("iota_row", [P, P], BF16)
        iota_blk = sb("iota_blk", [P, NB], BF16)
        first_slot = sb("first_slot", [P, NB])
        unused_row = sb("unused_row", [P, NB])
        tile_no = sb("tile_no", [P, NT])
        row_code = sb("row_code", [P, K])
        e8 = sb("e8", [P, NT, 8])
        ex8 = sb("ex8", [P, NT, 8])
        den = sb("den", [P, NT])
        rden = sb("rden", [P, NT])
        pick = [sb(f"pick{k}", [P, NT, E]) for k in range(K)]
        both = sb("both", [P, NT, E], BF16)
        cnt = sb("cnt", [P, E])
        cnt_i = [sb(f"cnt_i{n}", [P, E], I32) for n in range(2)]
        padded = sb("padded", [P, E])
        end = sb("end", [P, E])
        start = sb("start", [P, E])
        upto = sb("upto", [P, NT, E])
        pos = [sb(f"pos{n}", [P, NT, E]) for n in range(2)]
        hit = sb("hit", [P, NT, E])
        slot = sb("slot", [P, NT, K])
        slot_i = sb("slot_i", [P, NK], I32)
        slot_b = sb("slot_b", [P, NK], I32)
        slot_r = sb("slot_r", [P, NK], I32)
        blk = sb("blk", [P, NK])
        row = sb("row", [P, NK])
        own = [sb(f"own{n}", [P, NB]) for n in range(2)]
        oh_row = [sb(f"oh_row{n}", [P, P], BF16) for n in range(4)]
        oh_blk = [sb(f"oh_blk{n}", [P, 2, NB], BF16) for n in range(4)]
        sg = [sb(f"sg{n}", [P, GN]) for n in range(2)]
        hT = [sb(f"hT{n}", [P, FC, GN]) for n in range(2)]
        tab = [sb(f"tab{n}", [P, NB]) for n in range(5)]
        x2T = [sb(f"r_x2T{n}", [P, GN]) for n in range(2)]

        consts = sem("r_consts")
        x_ld = [sem(f"r_x_ld{n}") for n in range(2)]
        exp_in = sem("r_exp_in")
        exp_ok = sem("r_exp_ok")
        both_ok = sem("r_both_ok")
        ranks_ps = sem("r_ranks_ps")
        pos_ok = sem("r_pos_ok")
        oh_ok = sem("r_oh_ok")
        oh_used = sem("r_oh_used")
        g_ps = sem("r_g_ps")
        u_ps = sem("r_u_ps")
        sg_ok = sem("r_sg_ok")
        hT_ok = sem("r_hT_ok")
        o_ps = sem("r_o_ps")
        added = sem("r_added")
        dve_self = sem("r_dve_self")

        def table(ap):
            return ap[:, :].rearrange("p (t e) -> p t e", e=E)

        block = stack.enter_context(nc.Block())

        def groups(engine, step):
            for g in range(2):
                step(g, 0, g, True)
            with engine.Fori(1, NG // 2) as j:
                for par in range(2):
                    step(j * 2 + par, j, par, False)

        @block.sync
        def _(sp):
            def step(g, j, par, first):
                if not first:
                    sp.wait_ge(u_ps, (g - 1) * FC)
                sp.dma_start(x2T[par][:, :], x2T_cols[:, ds(g * GN, GN)]).then_inc(x_ld[par], 16)

            groups(sp, step)

        @block.gpsimd
        def _(pool):
            c = Done(pool, consts)

            def iota(to, pattern, base, each):
                c.add(nc.gpsimd.iota(to, pattern, base=base, channel_multiplier=each,
                                     allow_small_or_imprecise_dtypes=True))

            c.add(nc.gpsimd.memset(before_m[:, :], 1.0))
            c.add(nc.gpsimd.memset(ones_bf[:, :], 1.0))
            c.add(nc.gpsimd.memset(ones_f[:, :], 1.0))
            c.wait()
            c.add(nc.gpsimd.affine_select(out=before_m[:, :], in_=before_m[:, :], compare_op=ALU.is_gt, fill=0.0,
                                          base=0, pattern=[[1, P]], channel_multiplier=-1))
            iota(iota_e[:, :], [[1, E]], 0, 0)
            iota(iota_row[:, :], [[1, P]], 0, 0)
            iota(iota_blk[:, :], [[1, NB]], 0, 0)
            iota(first_slot[:, :], [[P, NB]], 0, 0)
            iota(unused_row[:, :], [[P, NB]], T * K + 1, 1)
            iota(tile_no[:, :], [[1, NT]], 0, 0)
            iota(row_code[:, :], [[1, K]], 1, K)
            assert c.n == R_CONSTS

        @block.tensor
        def _(pe):
            pe.wait_ge(consts, R_CONSTS)
            pe.wait_ge(both_ok, 1)
            flat = both[:, :, :].rearrange("p t e -> p (t e)")
            nc.tensor.matmul(bank[0][:, :], before_m[:, :], flat, start=True, stop=True)
            nc.tensor.matmul(bank[1][:, :], ones_bf[:, :], flat, start=True, stop=True).then_inc(ranks_ps, 1)
            pe.wait_ge(pos_ok, 1)

            def rows(g, par, first):
                pe.wait_ge(hT_ok, (g + 1) * FC)
                if not first:
                    pe.wait_ge(added, g)
                for t in range(GT):
                    for c in range(FC):
                        last = nc.tensor.matmul(bank[4 + par][:, t * P:(t + 1) * P], hT[par][:, c, t * P:(t + 1) * P],
                                                w2[:, SHARED, c * D:(c + 1) * D], start=(c == 0), stop=(c == FC - 1))
                last.then_inc(o_ps, 1)

            def table_of(n, c, start):
                for q in range(c * OC, (c + 1) * OC):
                    pe.wait_ge(oh_ok, n * OC + q % OC + 1)
                    nc.tensor.matmul(bank[6][:, 0:2 * NB], oh_row[q % 4][:, :],
                                     oh_blk[q % 4][:, :, :].rearrange("p a n -> p (a n)"),
                                     start=start and q == 0, stop=True, skip_group_check=True).then_inc(oh_used, 1)

            def step(g, j, par, first):
                pe.wait_ge(x_ld[par], 16 if first else 16 * (j + 1))
                for c in range(FC):
                    n = g * FC + c
                    for ps, done, w, b, used in ((g_ps, sg_ok, w1, 0, sg_ok), (u_ps, hT_ok, w3, 2, hT_ok)):
                        if not (first and par == 0 and c < 2):
                            pe.wait_ge(used, n - 1)
                        nc.tensor.matmul(bank[b + c % 2][:, :], w[:, SHARED, c * P:(c + 1) * P],
                                         x2T[par][:, :], start=True, stop=True).then_inc(ps, 1)
                    if not (first and par == 0 and c == 0):
                        table_of(n - 1, (c - 1) % FC, first and par == 0 and c == 1)
                    if c == 1 and not (first and par == 0):
                        rows(g - 1, 1 - par, first)

            groups(pe, step)
            table_of(NG * FC - 1, FC - 1, False)
            rows(NG - 1, 1, False)

        @block.scalar
        def _(act):
            act.wait_ge(exp_in, 1)
            nc.scalar.activation(ex8[:, :, :], e8[:, :, :], ACT.Exp).then_inc(exp_ok, 1)

            def step(g, j, par, first):
                for c in range(FC):
                    n = g * FC + c
                    act.wait_ge(g_ps, n + 1)
                    if not (first and par == 0 and c < 2):
                        act.wait_ge(hT_ok, n - 1)
                    nc.scalar.activation(sg[c % 2][:, :], bank[c % 2][:, :], ACT.Silu).then_inc(sg_ok, 1)

            groups(act, step)

        @block.vector
        def _(dve):
            c = Done(dve, dve_self)
            dve.wait_ge(consts, R_CONSTS)
            for k in range(K):
                c.add(nc.vector.tensor_tensor(pick[k][:, :, :], across(iota_e[:, :], NT), over(top_i[:, :, k], E),
                                              ALU.is_equal))
            c.wait()
            nc.vector.tensor_tensor(both[:, :, :], pick[0][:, :, :], pick[1][:, :, :], ALU.add).then_inc(both_ok, 1)
            nc.vector.tensor_tensor(e8[:, :, :], top_v[:, :, :], over(top_v[:, :, 0], 8),
                                    ALU.subtract).then_inc(exp_in, 1)
            dve.wait_ge(ranks_ps, 1)
            c.link(nc.vector.reduce_sum(cnt[:, :], table(bank[1]).rearrange("p t e -> p e t"), AX.X))
            c.link(nc.vector.tensor_scalar(cnt_i[0][:, :], cnt[:, :], float(P - 1), None, ALU.add))
            shift = P.bit_length() - 1
            c.link(nc.vector.tensor_scalar(cnt_i[1][:, :], cnt_i[0][:, :], shift, shift,
                                           ALU.logical_shift_right, ALU.logical_shift_left))
            c.link(nc.vector.tensor_copy(padded[:, :], cnt_i[1][:, :]))
            c.link(nc.vector.tensor_tensor_scan(end[:, :], ones_f[:, 0:E], padded[:, :], 0.0, ALU.mult, ALU.add))
            c.link(nc.vector.tensor_tensor(start[:, :], end[:, :], padded[:, :], ALU.subtract))
            for e in range(E):
                c.add(nc.vector.tensor_tensor_scan(upto[:, :, e], ones_f[:, :], table(bank[1])[:, :, e],
                                                   start[:, e:e + 1], ALU.mult, ALU.add))
            c.wait()
            c.link(nc.vector.tensor_tensor(pos[0][:, :, :], table(bank[1]), upto[:, :, :], ALU.subtract))
            nc.vector.tensor_tensor(pos[1][:, :, :], table(bank[0]), pos[0][:, :, :],
                                    ALU.subtract).then_inc(pos_ok, 1)
            dve.wait_ge(pos_ok, 1)
            for k in range(K):
                c.link(nc.vector.tensor_tensor(hit[:, :, :], pick[k][:, :, :], pos[1][:, :, :], ALU.mult))
                c.link(nc.vector.reduce_sum(slot[:, :, k], hit[:, :, :], AX.X))
            c.link(nc.vector.tensor_copy(slot_i[:, :], slot[:, :, :].rearrange("p t k -> p (t k)")))
            c.add(nc.vector.tensor_scalar(slot_b[:, :], slot_i[:, :], shift, None, ALU.logical_shift_right))
            c.add(nc.vector.tensor_scalar(slot_r[:, :], slot_i[:, :], P - 1, None, ALU.bitwise_and))
            c.wait()
            c.add(nc.vector.tensor_copy(blk[:, :], slot_b[:, :]))
            c.add(nc.vector.tensor_copy(row[:, :], slot_r[:, :]))
            c.wait()
            assert c.n == R_SELF

            def one_hots(g, c, first):
                for q in range(c * OC, (c + 1) * OC):
                    n = g * OH + q
                    if not (first and q < 4):
                        dve.wait_ge(oh_used, n - 3)
                    nc.vector.tensor_scalar(oh_row[q % 4][:, :], iota_row[:, :], row[:, ds(n, 1)], None, ALU.is_equal)
                    nc.vector.tensor_scalar(oh_blk[q % 4][:, 0, :], iota_blk[:, :], blk[:, ds(n, 1)],
                                            row_code[:, q % K:q % K + 1], ALU.is_equal, ALU.mult)
                    nc.vector.tensor_scalar(oh_blk[q % 4][:, 1, :], iota_blk[:, :], blk[:, ds(n, 1)],
                                            tile_no[:, ds(g * GT + q // K, 1)], ALU.is_equal, ALU.mult
                                            ).then_inc(oh_ok, 1)

            def add(g, par):
                dve.wait_ge(o_ps, g + 1)
                at = x2_all[:, ds(g * GT, GT), :].rearrange("p t d -> p (t d)")
                nc.vector.scalar_tensor_tensor(at, bank[4 + par][:, :], ALPHA / NS, at, ALU.mult,
                                               ALU.add).then_inc(added, 1)

            def step(g, j, par, first):
                for c in range(FC):
                    n = g * FC + c
                    dve.wait_ge(sg_ok, n + 1)
                    dve.wait_ge(u_ps, n + 1)
                    nc.vector.tensor_tensor(hT[par][:, c, :], sg[c % 2][:, :], bank[2 + c % 2][:, :],
                                            ALU.mult).then_inc(hT_ok, 1)
                    if c == 2 and not (first and par == 0):
                        add(g - 1, 1 - par)
                    one_hots(g, c, first and par == 0)

            groups(dve, step)
            add(NG - 1, 1)
            dve.wait_ge(exp_ok, 1)
            c.link(nc.vector.reduce_sum(den[:, :], ex8[:, :, :], AX.X))
            c.link(nc.vector.reciprocal(rden[:, :], den[:, :]))
            for k in range(K):
                c.add(nc.vector.scalar_tensor_tensor(gates[:, k, :], rden[:, :], 1.0 - ALPHA, ex8[:, :, k],
                                                     ALU.mult, ALU.mult))
            c.add(nc.vector.memset(own[0][:, :], 0.0))
            c.wait()
            for e in range(E - 1):
                c.link(nc.vector.scalar_tensor_tensor(own[(e + 1) % 2][:, :], first_slot[:, :], end[:, e:e + 1],
                                                      own[e % 2][:, :], ALU.is_ge, ALU.add))
            c.add(nc.vector.tensor_scalar(w_at[:, :], own[(E - 1) % 2][:, :], float(F), None, ALU.mult))
            code, empty, less, moved, src = tab
            dve.wait_ge(oh_used, NK)
            c.link(nc.vector.tensor_scalar(code[:, :], bank[6][:, NB:2 * NB], float(K * P), None, ALU.mult))
            c.link(nc.vector.tensor_tensor(less[:, :], bank[6][:, 0:NB], code[:, :], ALU.add))
            c.add(nc.vector.tensor_scalar(empty[:, :], less[:, :], 0.0, None, ALU.is_equal))
            c.add(nc.vector.tensor_scalar(src[:, :], less[:, :], 1.0, 0.0, ALU.subtract, ALU.max))
            c.wait()
            c.link(nc.vector.tensor_tensor(moved[:, :], empty[:, :], unused_row[:, :], ALU.mult))
            c.link(nc.vector.scalar_tensor_tensor(code[:, :], less[:, :], -1.0, moved[:, :], ALU.add, ALU.add))
            c.add(nc.vector.tensor_copy(dst_tab[:, :], code[:, :]))
            c.link(nc.vector.tensor_copy(src_tab[:, :], src[:, :]))
            c.link(nc.vector.tensor_scalar(src_tab[:, :], src_tab[:, :], K.bit_length() - 1, None,
                                           ALU.logical_shift_right))


R_CONSTS = 11
R_SELF = 2 + 6 + E + 1 + 2 * K + 1 + 4


def experts(nc, sem, bank, m):
    w1, w3, w2, ident = m["w1"], m["w3"], m["w2"], m["ident"]
    src_tab, dst_tab, w_at = m["src_tab"], m["dst_tab"], m["w_at"]
    x2_rows, y_rows = m["x2_rows"], m["y_rows"]
    stack = ExitStack()
    with stack:
        def sb(name, shape, dt=F32):
            return stack.enter_context(nc.sbuf_tensor(name, shape, dt))

        src = [sb(f"src{n}", [P, 1], U32) for n in range(2)]
        dst = [sb(f"dst{n}", [P, 1], U32) for n in range(2)]
        xg = [sb(f"xg{n}", [P, D]) for n in range(2)]
        xT = [sb(f"e_xT{n}", [P, P]) for n in range(2)]
        sg = [sb(f"e_sg{n}", [P, F]) for n in range(2)]
        h = [sb(f"e_h{n}", [P, F]) for n in range(2)]
        hT = [sb(f"e_hT{n}", [P, F]) for n in range(2)]
        y = [sb(f"e_y{n}", [P, D]) for n in range(2)]

        src_ok = sem("e_src_ok")
        gathered = [sem(f"e_gathered{n}") for n in range(2)]
        scattered = [sem(f"e_scattered{n}") for n in range(2)]
        xT_ps = sem("e_xT_ps")
        xT_ok = sem("e_xT_ok")
        g_ps = sem("e_g_ps")
        u_ps = sem("e_u_ps")
        sg_ok = sem("e_sg_ok")
        h_ok = sem("e_h_ok")
        hT_ps = sem("e_hT_ps")
        hT_ok = sem("e_hT_ok")
        y_ps = sem("e_y_ps")
        y_ok = sem("e_y_ok")

        block = stack.enter_context(nc.Block())

        def steps(engine, step):
            for b in range(4):
                step(b, b // 2, b % 2)
            with engine.Fori(2, NB // 2 - 2) as j:
                for par in range(2):
                    step(j * 2 + par, j, par, inner=True)
            for b in range(NB - 4, NB + 2):
                step(b, b // 2, b % 2)

        @block.gpsimd
        def _(pool):
            src_turn = Turns(pool, src_ok, "n_src", 4 + 3 + 1)
            y_turn = Turns(pool, y_ok, "n_y", 2 + 1)

            def gather(b, par):
                src_turn.wait(b + 1)
                nc.gpsimd.indirect_dma_start(xg[par][:, :], None, x2_rows,
                                             bass.IndirectOffsetOnAxis(src[par][:, 0:1], 0)
                                             ).then_inc(gathered[par], 16)

            def scatter(b, par):
                y_turn.wait(b + 1)
                nc.gpsimd.indirect_dma_start(y_rows, bass.IndirectOffsetOnAxis(dst[par][:, 0:1], 0),
                                             y[par][:, :], None).then_inc(scattered[par], 16)

            for b in range(3):
                gather(b, b % 2)

            def step(b, j, par, inner=False):
                if inner or b >= 2:
                    scatter(b - 2, par)
                if inner or b + 3 < NB:
                    gather(b + 3, 1 - par)

            steps(pool, step)
            for n in range(2):
                pool.wait_ge(scattered[n], 16 * (NB // 2))

        @block.tensor
        def _(pe):
            at_reg = [pe.alloc_register(f"w_at{n}") for n in range(2)]

            def look_up(b, par):
                pe.reg_mov(at_reg[par], pe.value_load(w_at[0:1, ds(b, 1)], min_val=0, max_val=(E - 1) * F))

            def weights_at(par):
                return pe.snap(at_reg[par], min_val=0, max_val=(E - 1) * F)

            def columns(w, at, n):
                return w[:, :, :].rearrange("p e f -> p (e f)")[:, ds(at, n)]

            def transpose_x(par, gathers):
                pe.wait_ge(gathered[par], 16 * gathers)
                nc.tensor.transpose(bank[7][:, 0:P], xg[par][:, :], ident[:, :]).then_inc(xT_ps, 1)

            look_up(0, 0)
            transpose_x(0, 1)

            def step(b, j, par, inner=False):
                other = 1 - par
                if inner or b < NB:
                    at = weights_at(par)
                if inner or 1 <= b <= NB:
                    before = weights_at(other)
                if inner or b < NB:
                    pe.wait_ge(xT_ok, b + 1)
                    if inner or b >= 2:
                        pe.wait_ge(sg_ok, b - 1)
                    nc.tensor.matmul(bank[par][:, :], xT[par][:, :], columns(w1, at, F),
                                     start=True, stop=True).then_inc(g_ps, 1)
                if inner or b + 1 < NB:
                    look_up(b + 1, other)
                    transpose_x(other, j + 1 + par)
                if inner or 1 <= b <= NB:
                    pe.wait_ge(h_ok, b)
                    for c in range(FC):
                        last = nc.tensor.transpose(bank[4 + other][:, c * P:(c + 1) * P],
                                                   h[other][:, c * P:(c + 1) * P], ident[:, :])
                    last.then_inc(hT_ps, 1)
                if inner or b < NB:
                    nc.tensor.matmul(bank[2 + par][:, :], xT[par][:, :], columns(w3, at, F),
                                     start=True, stop=True).then_inc(u_ps, 1)
                if inner or 1 <= b <= NB:
                    pe.wait_ge(hT_ok, b)
                    if inner or b >= 2:
                        pe.wait_ge(y_ok, b - 1)
                    for c in range(FC):
                        last = nc.tensor.matmul(bank[6][:, 0:D], hT[other][:, c * P:(c + 1) * P],
                                                columns(w2, before + c * D, D), start=(c == 0), stop=(c == FC - 1))
                    last.then_inc(y_ps, 1)

            steps(pe, step)

        @block.scalar
        def _(act):
            def step(b, j, par, inner=False):
                other = 1 - par
                if inner or b < NB:
                    act.wait_ge(g_ps, b + 1)
                    if inner or b >= 2:
                        act.wait_ge(h_ok, b - 1)
                    nc.scalar.activation(sg[par][:, :], bank[par][:, :], ACT.Silu).then_inc(sg_ok, 1)
                if inner or 1 <= b <= NB:
                    act.wait_ge(hT_ps, b)
                    nc.scalar.activation(hT[other][:, :], bank[4 + other][:, :], ACT.Copy).then_inc(hT_ok, 1)

            steps(act, step)

        @block.vector
        def _(dve):
            def stage(b, par):
                nc.vector.tensor_copy(src[par][:, :], src_tab[:, ds(b, 1)]).then_inc(src_ok, 1)

            def take_x(b, par):
                dve.wait_ge(xT_ps, b + 1)
                nc.vector.tensor_copy(xT[par][:, :], bank[7][:, 0:P]).then_inc(xT_ok, 1)

            stage(0, 0)
            stage(1, 1)
            take_x(0, 0)
            stage(2, 0)

            def step(b, j, par, inner=False):
                other = 1 - par
                if inner or b >= 2:
                    dve.wait_ge(y_ps, b - 1)
                    if inner or b >= 4:
                        dve.wait_ge(scattered[par], 16 * (j - 1))
                    nc.vector.tensor_copy(dst[par][:, :], dst_tab[:, ds(b - 2, 1)])
                    nc.vector.tensor_copy(y[par][:, :], bank[6][:, 0:D]).then_inc(y_ok, 1)
                if inner or b + 1 < NB:
                    take_x(b + 1, other)
                if inner or b + 3 < NB:
                    stage(b + 3, other)
                if inner or b < NB:
                    dve.wait_ge(sg_ok, b + 1)
                    dve.wait_ge(u_ps, b + 1)
                    nc.vector.tensor_tensor(h[par][:, :], sg[par][:, :], bank[2 + par][:, :],
                                            ALU.mult).then_inc(h_ok, 1)

            steps(dve, step)


def combine(nc, sem, bank, m):
    x2_all, gates, minus_half, y_rows, out_rows = m["x2_all"], m["gates"], m["minus_half"], m["y_rows"], m["out_rows"]
    group_rows = m["group_rows"]
    stack = ExitStack()
    with stack:
        def sb(name, shape, dt=F32):
            return stack.enter_context(nc.sbuf_tensor(name, shape, dt))

        yk = [sb(f"yk{n}", [P, GT, K, D]) for n in range(2)]
        part = sb("part", [P, GT, D])
        z = [sb(f"z{n}", [P, GT, D]) for n in range(2)]
        res = [sb(f"res{n}", [P, GT, D]) for n in range(2)]
        st = sb("f_st", [P, GT, 6])
        mv = [sb(f"f_mv{n}", [P, GT, 2]) for n in range(2)]
        ve = [sb(f"f_ve{n}", [P, GT]) for n in range(2)]
        rs = [sb(f"f_rs{n}", [P, GT]) for n in range(2)]

        y_ld = [sem(f"f_y_ld{n}") for n in range(2)]
        stored = [sem(f"f_stored{n}") for n in range(2)]
        z_ok = sem("f_z_ok")
        ve_ok = sem("f_ve_ok")
        rs_ok = sem("f_rs_ok")
        res_ok = sem("f_res_ok")
        st_ok = sem("f_st_ok")
        dve_self = sem("f_dve_self")

        block = stack.enter_context(nc.Block())
        both = y_rows[0:T * K, :].rearrange("(n k) d -> n (k d)", k=K)

        @block.sync
        def _(sp):
            def load(g, par):
                sp.dma_start(yk[par][:, :, :, :].rearrange("p t k d -> p t (k d)"),
                             both[ds(g * GN, GN), :].rearrange("(t p) d -> p t d", p=P)).then_inc(y_ld[par], 16)

            for g in range(2):
                load(g, g)
            with sp.Fori(1, NG // 2) as j:
                for par in range(2):
                    g = j * 2 + par
                    sp.wait_ge(z_ok, g - 1)
                    load(g, par)

        @block.gpsimd
        def _(pool):
            with pool.Fori(0, NG // 2) as j:
                for par in range(2):
                    pool.wait_ge(ve_ok, j * 2 + par + 1)
                    nc.gpsimd.tensor_tensor(rs[par][:, :], ve[par][:, :], minus_half[:, 0:GT],
                                            ALU.pow).then_inc(rs_ok, 1)

        @block.vector
        def _(dve):
            st_turn = Turns(dve, st_ok, "n_f_st", 4)

            def sums(g, j, par, before):
                c = Done(dve, dve_self, before)
                dve.wait_ge(y_ld[par], 16 * (j + 1))
                for t in range(GT):
                    c.add(nc.vector.scalar_tensor_tensor(part[:, t, :], yk[par][:, t, 0, :],
                                                         gates[:, 0, ds(g * GT + t, 1)],
                                                         x2_all[:, ds(g * GT + t, 1), :].rearrange("p a d -> p (a d)"),
                                                         ALU.mult, ALU.add))
                c.wait()
                for t in range(GT):
                    last = nc.vector.scalar_tensor_tensor(z[par][:, t, :], yk[par][:, t, 1, :],
                                                          gates[:, 1, ds(g * GT + t, 1)], part[:, t, :],
                                                          ALU.mult, ALU.add)
                last.then_inc(z_ok, 1)
                dve.wait_ge(z_ok, g + 1)
                for t in range(GT):
                    last = nc.vector.bn_stats(st[:, t, :], z[par][:, t, :])
                last.then_inc(st_ok, 1)
                st_turn.wait(g + 1)
                for t in range(GT):
                    c.add(nc.vector.bn_aggr(mv[par][:, t, :], st[:, t, :]))
                c.wait()
                nc.vector.tensor_scalar(ve[par][:, :], mv[par][:, :, 1], EPS, None, ALU.add).then_inc(ve_ok, 1)
                assert c.n == N_SUMS

            def normalise(g, j, par, early):
                dve.wait_ge(rs_ok, g + 1)
                if not early:
                    dve.wait_ge(stored[par], 16 * j)
                for t in range(GT):
                    last = nc.vector.tensor_scalar(res[par][:, t, :], z[par][:, t, :], mv[par][:, t, 0:1],
                                                   rs[par][:, t:t + 1], ALU.subtract, ALU.mult)
                last.then_inc(res_ok, 1)

            sums(0, 0, 0, 0)
            sums(1, 0, 1, N_SUMS)
            normalise(0, 0, 0, True)
            sums(2, 1, 0, 2 * N_SUMS)
            normalise(1, 0, 1, True)
            with dve.Fori(1, NG // 2 - 1) as j:
                sums(j * 2 + 1, j, 1, (j * 2 + 1) * N_SUMS)
                normalise(j * 2, j, 0, False)
                sums(j * 2 + 2, j + 1, 0, (j * 2 + 2) * N_SUMS)
                normalise(j * 2 + 1, j, 1, False)
            j = NG // 2 - 1
            sums(NG - 1, j, 1, (NG - 1) * N_SUMS)
            normalise(NG - 2, j, 0, False)
            normalise(NG - 1, j, 1, False)

        @block.scalar
        def _(act):
            with act.Fori(0, NG // 2) as j:
                for par in range(2):
                    g = j * 2 + par
                    act.wait_ge(res_ok, g + 1)
                    act.dma_start(group_rows(out_rows, g), res[par][:, :, :]).then_inc(stored[par], 16)
            for n in range(2):
                act.wait_ge(stored[n], 16 * (NG // 2))


N_SUMS = 2 * GT

_INS = ["x", "ctx_1024", "L0_attn_Wq", "L0_attn_bq", "L0_attn_Wk", "L0_attn_bk", "L0_attn_Wv", "L0_attn_bv",
        "L0_ffn_gate_W", "L0_ffn_w1_e", "L0_ffn_w3_e", "L0_ffn_w2_e", "L0_ffn_w1_s", "L0_ffn_w3_s", "L0_ffn_w2_s"]


def kernel(**inputs):
    import numpy as _np
    import concourse.bacc as _bacc
    from concourse import mybir as _mybir
    from concourse.bass_utils import run_bass_kernel_spmd as _run

    nc = _bacc.Bacc("TRN2", target_bir_lowering=False, num_devices=1)
    arrays, args = {}, []
    for name in _INS:
        a = _np.ascontiguousarray(inputs[name])
        arrays[f"in_{name}_dram"] = a
        args.append(nc.dram_tensor(f"in_{name}_dram", a.shape, _mybir.dt.from_np(a.dtype), kind="ExternalInput").ap())
    out = nc.dram_tensor("out_0_dram", (B, S, D), _mybir.dt.float32, kind="ExternalOutput").ap()
    decoder(nc, *args, out)
    r = _run(nc, [arrays], core_ids=[0])
    return r.results[0]["out_0_dram"]
```

```python
from contextlib import ExitStack

import concourse.bass as bass
from concourse import mybir

F32 = mybir.dt.float32
F32R = mybir.dt.float32r
BF16 = mybir.dt.bfloat16
I32 = mybir.dt.int32
U32 = mybir.dt.uint32
ACT = mybir.ActivationFunctionType
ALU = mybir.AluOpType
AX = mybir.AxisListType
ds = bass.ds

P = 128
B, S, D = 128, 64, 128
T = B * S
GT = 4
GN = GT * P
NG = T // GN
NT = T // P
GB = GN // S
E, F, K = 8, 512, 2
FC = F // P
NS, FS = 8, 64
SHARED = E
NB = T * K // P + E
EPS = 1e-5
Q_SCALE = float(D) ** -0.5
X_SCALE = 1.0 / S
ALPHA = 0.5
assert NS * FS == F and 2 * FC == E and NB % 2 == 0 and NG % 2 == 0 and NT <= 256 and 2 * P <= 256 and NB <= 256


class Done:

    def __init__(self, engine, sem, before=0):
        self.engine, self.sem, self.before, self.n = engine, sem, before, 0

    def add(self, instruction):
        self.n += 1
        return instruction.then_inc(self.sem, 1)

    def wait(self):
        self.engine.wait_ge(self.sem, self.before + self.n)

    def link(self, instruction):
        self.add(instruction)
        self.wait()


class Turns:

    def __init__(self, engine, sem, name, first):
        self.engine, self.sem, self.count = engine, sem, engine.alloc_register(name)
        engine.reg_mov(self.count, first)

    def wait(self, value):
        if isinstance(value, int):
            self.engine.wait_ge(self.sem, value)
        else:
            self.engine.wait_ge(self.sem, self.engine.snap(self.count))
            self.engine.reg_add(self.count, self.count, 1)


def over(ap, n):
    return ap.unsqueeze(2).broadcast_to([ap.shape[0], ap.shape[1], n])


def across(ap, n):
    return ap.unsqueeze(1).broadcast_to([ap.shape[0], n, ap.shape[1]])


def decoder(nc, x, ctx, wq, bq, wk, bk, wv, bv, gate_w, w1_e, w3_e, w2_e, w1_s, w3_s, w2_s, out):
    stack = ExitStack()
    with stack:
        def sb(name, shape, dt=F32):
            return stack.enter_context(nc.sbuf_tensor(name, shape, dt))

        def sem(name):
            return stack.enter_context(nc.semaphore(name))

        bank = [stack.enter_context(nc.psum_tensor(f"bank{i}", [P, 512], F32)) for i in range(8)]

        x_rows = x.rearrange("b s d -> (b s) d")
        ctx_rows = ctx.rearrange("b s d -> (b s) d")
        out_rows = out.rearrange("b s d -> (b s) d")
        x2_rows = nc.dram_tensor("x2_rows", (T, D), F32, kind="Internal").ap()
        x2T_cols = nc.dram_tensor("x2T_cols", (D, T), F32, kind="Internal").ap()
        y_rows = nc.dram_tensor("y_rows", (T * K + NB * P, D), F32, kind="Internal").ap()

        def group_rows(rows, g):
            return rows[ds(g * GN, GN), :].rearrange("(j p) d -> p j d", p=P)

        w_hi = sb("w_hi", [P, E + 1, 2, F], F32R)
        w_lo = sb("w_lo", [P, E + 1, 2, F], F32R)
        w2 = sb("w2", [P, E + 1, F])
        ident = sb("ident", [P, P])
        top_v = sb("top_v", [P, NT, 8])
        top_i = sb("top_i", [P, NT, K])
        gates = sb("gates", [P, K, NT])
        src_tab = sb("src_tab", [P, NB], U32)
        dst_tab = sb("dst_tab", [P, NB], U32)
        w_at = sb("w_at", [P, NB], I32)
        minus_half = sb("minus_half", [P, 2 * GT])
        iota_e = sb("iota_e", [P, E])
        before_m = sb("before_m", [P, P], BF16)
        ones_bf = sb("ones_bf", [P, P], BF16)
        ones_f = sb("ones_f", [P, NT])
        iota_row = sb("iota_row", [P, P], BF16)
        iota_blk = sb("iota_blk", [P, NB], BF16)
        first_slot = sb("first_slot", [P, NB])
        unused_row = sb("unused_row", [P, NB])
        tile_no = sb("tile_no", [P, NT])
        row_code = sb("row_code", [P, K])

        attention(nc, sem, bank, locals())
        x2_all = sb("x2_all", [P, NT, D])
        routing(nc, sem, bank, locals())
        experts(nc, sem, bank, locals())
        combine(nc, sem, bank, locals())


def attention(nc, sem, bank, m):
    bk, bv, bq, gate_w = m["bk"], m["bv"], m["bq"], m["gate_w"]
    iota_e, before_m, ones_bf, ones_f = m["iota_e"], m["before_m"], m["ones_bf"], m["ones_f"]
    iota_row, iota_blk, first_slot = m["iota_row"], m["iota_blk"], m["first_slot"]
    unused_row, tile_no, row_code = m["unused_row"], m["tile_no"], m["row_code"]
    group_rows, x_rows, ctx_rows = m["group_rows"], m["x_rows"], m["ctx_rows"]
    x2_rows, x2T_cols = m["x2_rows"], m["x2T_cols"]
    w_hi, w_lo, w2, ident = m["w_hi"], m["w_lo"], m["w2"], m["ident"]
    top_v, top_i, minus_half = m["top_v"], m["top_i"], m["minus_half"]
    stack = ExitStack()
    with stack:
        def sb(name, shape, dt=F32):
            return stack.enter_context(nc.sbuf_tensor(name, shape, dt))

        def pair(name, shape, dt=F32):
            return [sb(f"{name}{n}", shape, dt) for n in range(2)]

        def sems(names):
            return [sem(n) for n in names.split()]

        w_raw = sb("w_raw", [P, 3, D])
        gw_raw = sb("gw_raw", [E, D])
        wT = sb("wT", [P, 3, D])
        gwT = sb("gwT", [P, E])
        bq_row = sb("bq_row", [1, GT, D])
        ones_row = sb("ones_row", [1, P])
        bkv = sb("bkv", [P, 2])
        mask_a = sb("mask_a", [P, P])
        x_in = pair("x_in", [P, GT, D])
        x_res = pair("x_res", [P, GT, D])
        c_in = pair("c_in", [P, GT, D])
        w_in = pair("w_in", [P, 2, F])
        xT = sb("xT", [P, GN])
        cT = sb("cT", [P, GN])
        x1T = sb("x1T", [P, GN])
        x2T = pair("x2T", [P, GN])
        eq = sb("eq", [P, GT, D])
        ek = pair("ek", [P, GB, S])
        ev = sb("ev", [P, GB, S])
        qT = pair("qT", [P, GN])
        vn = sb("vn", [P, GB, S])
        v = pair("v", [P, GT, D])
        sc_a = sb("sc_a", [P, GT, P])
        sc_x = sb("sc_x", [P, GT, P])
        y1 = sb("y1", [P, GT, D])
        y2 = sb("y2", [P, GT, D])
        x1 = pair("x1_", [P, GT, D])
        x2 = pair("x2_", [P, GT, D])
        nmax = sb("nmax", [P, GT])
        kvmax = sb("kvmax", [P, 2, GB])
        kvbias = sb("kvbias", [P, 2, GB])
        sums = pair("sums", [P, GT + 2 * GB])
        rsum = pair("rsum", [P, GT + 2 * GB])
        st = pair("st", [P, GT, 6])
        mv = pair("mv", [P, GT, 2])
        ve = pair("ve", [P, GT])
        rs = pair("rs", [P, GT])
        vs = sb("vs", [P, GT, 8])
        ix = sb("ix", [P, GT, 8], U32)

        small_in, bias_in, consts, wT_ps, wT_ok, hi_ok, lo_ok, w2_ld = sems(
            "small_in bias_in consts wT_ps wT_ok hi_ok lo_ok w2_ld")
        x_ld, r_ld, c_ld, w_ld, stored = (sems(f"{n}0 {n}1") for n in ("x_ld", "r_ld", "c_ld", "w_ld", "stored"))
        xT_ps, xT_ok, q_ps, k_ps, v_ps, qmax_ok, kmax_ok, vmax_ok, kbias_ok, vbias_ok = sems(
            "xT_ps xT_ok q_ps k_ps v_ps qmax_ok kmax_ok vmax_ok kbias_ok vbias_ok")
        eq_ok, ek_ok, ev_ok, rsum_ok, vn_ok, qT_ps, qT_ok, vT_ps, v_ok = sems(
            "eq_ok ek_ok ev_ok rsum_ok vn_ok qT_ps qT_ok vT_ps v_ok")
        sa_ps, sa_ok, o1_ps, cT_ps, cT_ok, x1T_ps, x1T_ok, sx_ps, sx_ok, o2_ps = sems(
            "sa_ps sa_ok o1_ps cT_ps cT_ok x1T_ps x1T_ok sx_ps sx_ok o2_ps")
        y_ok, st_ok, mv_ok, ve_ok, rs_ok, xn_ok = (
            sems(f"{n}1 {n}2") for n in ("y_ok", "st_ok", "mv_ok", "ve_ok", "rs_ok", "xn_ok"))
        x2T_ps, x2T_ok, l_ps, vs_ok, ix_ok, top_ok = sems("x2T_ps x2T_ok l_ps vs_ok ix_ok top_ok")

        def tiles(b):
            return bank[b][:, :].rearrange("p (j n) -> p j n", j=GT)

        def batches(b):
            return bank[b][:, :].rearrange("p (j n) -> p j n", j=GB)

        def later(g, n):
            return not isinstance(g, int) or g >= n

        def steps(engine, step, first, stages, split=None):
            def at_of(j, par, known):
                def at(s):
                    if known is not None and not 0 <= known - s < NG:
                        return None
                    return (j * 2 + par - s, j + (par - s) // 2, (par - s) % 2)
                return at

            for i in range(first):
                step(at_of(i // 2, i % 2, i))
                if split and i:
                    split(i - 1)
            with engine.Fori(first // 2, NG // 2) as j:
                for par in range(2):
                    step(at_of(j, par, None))
            for i in range(NG, NG + stages - 1):
                if split and i - NG + first - 1 <= E:
                    split(i - NG + first - 1)
                step(at_of(i // 2, i % 2, i))

        FIRST, STAGES = 6, 6
        assert FIRST - 1 + STAGES - 1 >= E + 1
        PROJECT, SOFTEN, MIX, CROSS, TURN, TOP = range(STAGES)

        block = stack.enter_context(nc.Block())

        @block.sync
        def _(sp):
            for n, w in enumerate((m["wq"], m["wk"], m["wv"])):
                sp.dma_start(w_raw[:, n, :], w).then_inc(small_in, 16)
            sp.dma_start(gw_raw[:, :], gate_w).then_inc(small_in, 16)

            def step(at):
                if now := at(0):
                    g, gj, gp = now
                    if later(g, 2):
                        sp.wait_ge(xT_ps, g - 1)
                    sp.dma_start(x_in[gp][:, :, :], group_rows(x_rows, g)).then_inc(x_ld[gp], 16)
                if now := at(6):
                    g, gj, gp = now
                    sp.wait_ge(x2T_ok, g + 1)
                    sp.dma_start(group_rows(x2_rows, g), x2[gp][:, :, :]).then_inc(stored[gp], 16)
                    sp.dma_start(x2T_cols[:, ds(g * GN, GN)], x2T[gp][:, :]).then_inc(stored[gp], 16)
                if now := at(2):
                    g, gj, gp = now
                    if later(g, 2):
                        sp.wait_ge(y_ok[0], g - 1)
                    sp.dma_start(x_res[gp][:, :, :], group_rows(x_rows, g)).then_inc(r_ld[gp], 16)
                if now := at(3):
                    g, gj, gp = now
                    if later(g, 2):
                        sp.wait_ge(o2_ps, g - 1)
                    sp.dma_start(c_in[gp][:, :, :], group_rows(ctx_rows, g)).then_inc(c_ld[gp], 16)

            def load(n):
                to = w_in[n % 2]
                if n >= 2:
                    sp.wait_ge(lo_ok, n - 1)
                if n < E:
                    parts = (m["w1_e"][n], m["w3_e"][n])
                else:
                    parts = (m["w1_s"].rearrange("n d f -> d n f"), m["w3_s"].rearrange("n d f -> d n f"))
                for k, part in enumerate(parts):
                    at = to[:, k, :] if n < E else to[:, k, :].rearrange("d (n f) -> d n f", n=NS)
                    sp.dma_start(at, part).then_inc(w_ld[n % 2], 16)
                rows = m["w2_e"][n] if n < E else m["w2_s"].rearrange("n f d -> (n f) d")
                sp.dma_start(w2[:, n, :].rearrange("p (c d) -> p c d", c=FC),
                              rows.rearrange("(c p) d -> p c d", p=P)).then_inc(w2_ld, 16)

            def prepare(n):
                if n == 0:
                    load(0)
                if n < E:
                    load(n + 1)

            steps(sp, step, FIRST, 7, prepare)
            for par in range(2):
                sp.wait_ge(stored[par], 32 * (NG // 2))

        @block.gpsimd
        def _(pool):
            c = Done(pool, consts)
            c.add(nc.gpsimd.memset(ident[:, :], 0.0))
            c.add(nc.gpsimd.memset(ones_row[:, :], 1.0))
            c.add(nc.gpsimd.memset(minus_half[:, :], -0.5))
            c.add(nc.gpsimd.memset(sc_x[:, :, :], 0.0))
            c.add(nc.gpsimd.memset(mask_a[:, :], 0.0))
            c.wait()
            c.link(nc.gpsimd.memset(mask_a[0:S, 0:S], Q_SCALE))
            c.link(nc.gpsimd.memset(mask_a[S:P, S:P], Q_SCALE))
            c.add(nc.gpsimd.affine_select(out=ident[:, :], in_=ident[:, :], compare_op=ALU.not_equal, fill=1.0,
                                          base=0, pattern=[[-1, P]], channel_multiplier=1))
            assert c.n == N_CONSTS

            def iota(to, pattern, base, each):
                c.add(nc.gpsimd.iota(to, pattern, base=base, channel_multiplier=each,
                                     allow_small_or_imprecise_dtypes=True))

            c.add(nc.gpsimd.memset(before_m[:, :], 1.0))
            c.add(nc.gpsimd.memset(ones_bf[:, :], 1.0))
            c.add(nc.gpsimd.memset(ones_f[:, :], 1.0))
            c.wait()
            c.add(nc.gpsimd.affine_select(out=before_m[:, :], in_=before_m[:, :], compare_op=ALU.is_gt, fill=0.0,
                                          base=0, pattern=[[1, P]], channel_multiplier=-1))
            iota(iota_e[:, :], [[1, E]], 0, 0)
            iota(iota_row[:, :], [[1, P]], 0, 0)
            iota(iota_blk[:, :], [[1, NB]], 0, 0)
            iota(first_slot[:, :], [[P, NB]], 0, 0)
            iota(unused_row[:, :], [[P, NB]], T * K + 1, 1)
            iota(tile_no[:, :], [[1, NT]], 0, 0)
            iota(row_code[:, :], [[1, K]], 1, K)
            def normalise(n, g, y, to):
                pool.wait_ge(ve_ok[n], g + 1)
                nc.gpsimd.tensor_tensor(rs[n][:, :], ve[n][:, :], minus_half[:, 0:GT], ALU.pow)
                nc.gpsimd.tensor_tensor(to[:, :, :], y[:, :, :], over(mv[n][:, :, 0], D),
                                        ALU.subtract).then_inc(rs_ok[n], 1)
                pool.wait_ge(rs_ok[n], g + 1)
                nc.gpsimd.tensor_tensor(to[:, :, :], to[:, :, :], over(rs[n][:, :], D),
                                        ALU.mult).then_inc(xn_ok[n], 1)

            def step(at):
                if now := at(MIX):
                    g, gj, gp = now
                    if later(g, 2):
                        pool.wait_ge(y_ok[1], g - 1)
                    normalise(0, g, y1, x1[gp])
                if now := at(SOFTEN):
                    g, gj, gp = now
                    pool.wait_ge(rsum_ok, g + 1)
                    nc.gpsimd.tensor_tensor(vn[:, :, :], ev[:, :, :], over(rsum[gp][:, GT + GB:], S),
                                            ALU.mult).then_inc(vn_ok, 1)
                if now := at(CROSS):
                    g, gj, gp = now
                    if later(g, 2):
                        pool.wait_ge(stored[gp], 32 * gj)
                    normalise(1, g, y2, x2[gp])

            steps(pool, step, FIRST, STAGES)

        @block.tensor
        def _(pe):
            pe.wait_ge(small_in, 16 * 4)
            pe.wait_ge(consts, N_CONSTS)
            for n in range(3):
                nc.tensor.transpose(bank[0][:, n * D:(n + 1) * D], w_raw[:, n, :], ident[:, :])
            nc.tensor.transpose(bank[0][:, 3 * D:3 * D + E], gw_raw[:, :], ident[0:E, 0:E]).then_inc(wT_ps, 1)
            pe.wait_ge(wT_ok, 1)
            pe.wait_ge(bias_in, 16 * 3)

            def transposes(b, of):
                for t in range(GT):
                    last = nc.tensor.transpose(bank[b][:, t * P:(t + 1) * P], of(t), ident[:, :])
                return last

            def products(b, lhsT, rhs):
                for t in range(GT):
                    last = nc.tensor.matmul(bank[b][:, t * P:(t + 1) * P], lhsT(t), rhs(t), start=True, stop=True)
                return last

            def two(ap, t):
                return ap[:, 2 * t:2 * t + 2, :].rearrange("p a s -> p (a s)")

            def step(at):
                project, soften, mix, cross, turn, top = (at(s) for s in range(STAGES))
                if project:
                    g, gj, gp = project
                    pe.wait_ge(x_ld[gp], 16 * (gj + 1))
                    if mix:
                        pe.wait_ge(qT_ok, g - 1)
                    elif soften:
                        pe.wait_ge(xT_ok, g)
                    transposes(0, lambda t: x_in[gp][:, t, :]).then_inc(xT_ps, 1)
                if cross:
                    g, gj, gp = cross
                    pe.wait_ge(c_ld[gp], 16 * (gj + 1))
                    if later(g, 1):
                        pe.wait_ge(sx_ok, g)
                    transposes(5, lambda t: c_in[gp][:, t, :]).then_inc(cT_ps, 1)
                if mix:
                    g, gj, gp = mix
                    pe.wait_ge(qT_ok, g + 1)
                    if later(g, 1):
                        pe.wait_ge(y_ok[0], g)
                    products(4, lambda t: two(ek[gp], t), lambda t: qT[gp][:, t * P:(t + 1) * P]).then_inc(sa_ps, 1)
                if cross:
                    g, gj, gp = cross
                    pe.wait_ge(xn_ok[0], g + 1)
                    if later(g, 1):
                        pe.wait_ge(y_ok[1], g)
                    transposes(6, lambda t: x1[gp][:, t, :]).then_inc(x1T_ps, 1)
                if mix:
                    g, gj, gp = mix
                    pe.wait_ge(vn_ok, g + 1)
                    if project:
                        pe.wait_ge(xT_ok, g + 3)
                    transposes(0, lambda t: two(vn, t)).then_inc(vT_ps, 1)
                if top:
                    g, gj, gp = top
                    pe.wait_ge(x2T_ok, g + 1)
                    for t in range(GT):
                        last = nc.tensor.matmul(bank[7][:, t * E:(t + 1) * E], x2T[gp][:, t * P:(t + 1) * P],
                                                gwT[:, :], start=True, stop=True)
                    last.then_inc(l_ps, 1)
                if cross:
                    g, gj, gp = cross
                    pe.wait_ge(cT_ok, g + 1)
                    pe.wait_ge(x1T_ok, g + 1)
                    products(5, lambda t: cT[:, t * P:(t + 1) * P],
                             lambda t: x1T[:, t * P:(t + 1) * P]).then_inc(sx_ps, 1)
                if mix:
                    g, gj, gp = mix
                    pe.wait_ge(v_ok, g + 1)
                    pe.wait_ge(sa_ok, g + 1)
                    products(4, lambda t: sc_a[:, t, :], lambda t: v[gp][:, t, :]).then_inc(o1_ps, 1)
                if project:
                    g, gj, gp = project
                    pe.wait_ge(xT_ok, g + 1)
                    if soften:
                        pe.wait_ge(eq_ok, g)
                    nc.tensor.matmul(bank[1][:, :], ones_row[:, :], bq_row[:, :, :].rearrange("a j d -> a (j d)"),
                                     start=True, stop=False)
                    for t in range(GT):
                        last = nc.tensor.matmul(bank[1][:, t * P:(t + 1) * P], xT[:, t * P:(t + 1) * P],
                                                wT[:, 0, :], start=False, stop=(t == GT - 1))
                    last.then_inc(q_ps, 1)
                if soften:
                    g, gj, gp = soften
                    pe.wait_ge(eq_ok, g + 1)
                    if mix:
                        pe.wait_ge(v_ok, g)
                    transposes(0, lambda t: eq[:, t, :]).then_inc(qT_ps, 1)
                if turn:
                    g, gj, gp = turn
                    pe.wait_ge(xn_ok[1], g + 1)
                    if later(g, 1):
                        pe.wait_ge(top_ok, g)
                    transposes(7, lambda t: x2[gp][:, t, :]).then_inc(x2T_ps, 1)
                if project:
                    g, gj, gp = project
                    if later(g, 1):
                        pe.wait_ge(ek_ok, g)
                    nc.tensor.matmul(bank[2][:, :], wT[:, 1, :], xT[:, :], start=True, stop=True).then_inc(k_ps, 1)
                if cross:
                    g, gj, gp = cross
                    pe.wait_ge(sx_ok, g + 1)
                    products(6, lambda t: sc_x[:, t, :], lambda t: c_in[gp][:, t, :]).then_inc(o2_ps, 1)
                if project:
                    g, gj, gp = project
                    if later(g, 1):
                        pe.wait_ge(ev_ok, g)
                    nc.tensor.matmul(bank[3][:, :], wT[:, 2, :], xT[:, :], start=True, stop=True).then_inc(v_ps, 1)


            steps(pe, step, FIRST, STAGES)

        @block.scalar
        def _(act):
            act.dma_start(bq_row[:, :, :], bq.rearrange("(a b n) -> a b n", a=1, b=1).broadcast_to([1, GT, D])
                          ).then_inc(bias_in, 16)
            act.dma_start(bkv[:, 0:1], bk.rearrange("(n a) -> n a", a=1)).then_inc(bias_in, 16)
            act.dma_start(bkv[:, 1:2], bv.rearrange("(n a) -> n a", a=1)).then_inc(bias_in, 16)
            act.wait_ge(wT_ps, 1)
            nc.scalar.activation(wT[:, :, :].rearrange("p a d -> p (a d)"), bank[0][:, 0:3 * D], ACT.Copy)
            nc.scalar.activation(gwT[:, :], bank[0][:, 3 * D:3 * D + E], ACT.Copy).then_inc(wT_ok, 1)

            def split_hi(n):
                act.wait_ge(w_ld[n % 2], 32 * (n // 2 + 1))
                nc.scalar.activation(w_hi[:, n, :, :], w_in[n % 2][:, :, :], ACT.Copy).then_inc(hi_ok, 1)


            def exps(n, e, gp):
                for b in range(GB):
                    col = GT + n * GB + b
                    last = nc.scalar.activation(e[:, b, :], batches(2 + n)[:, b, :], ACT.Exp,
                                                bias=kvbias[:, n, b:b + 1], accum_out=sums[gp][:, col:col + 1])
                return last

            def step(at):
                project, soften, mix, cross, turn, top = (at(s) for s in range(STAGES))
                if soften:
                    g, gj, gp = soften
                    act.wait_ge(qmax_ok, g + 1)
                    if later(g, 1):
                        act.wait_ge(qT_ps, g)
                    for t in range(GT):
                        last = nc.scalar.activation(eq[:, t, :], tiles(1)[:, t, :], ACT.Exp, bias=nmax[:, t:t + 1],
                                                    accum_out=sums[gp][:, t:t + 1])
                    last.then_inc(eq_ok, 1)
                if project:
                    g, gj, gp = project
                    act.wait_ge(xT_ps, g + 1)
                    nc.scalar.activation(xT[:, :], bank[0][:, :], ACT.Copy).then_inc(xT_ok, 1)
                if cross:
                    g, gj, gp = cross
                    act.wait_ge(cT_ps, g + 1)
                    nc.scalar.activation(cT[:, :], bank[5][:, :], ACT.Copy).then_inc(cT_ok, 1)
                    act.wait_ge(x1T_ps, g + 1)
                    nc.scalar.activation(x1T[:, :], bank[6][:, :], ACT.Copy).then_inc(x1T_ok, 1)
                if mix:
                    g, gj, gp = mix
                    act.wait_ge(vT_ps, g + 1)
                    nc.scalar.activation(v[gp][:, :, :].rearrange("p t d -> p (t d)"), bank[0][:, :],
                                         ACT.Copy).then_inc(v_ok, 1)
                if soften:
                    g, gj, gp = soften
                    act.wait_ge(kbias_ok, g + 1)
                    exps(0, ek[gp], gp).then_inc(ek_ok, 1)
                if cross:
                    g, gj, gp = cross
                    act.wait_ge(sx_ps, g + 1)
                    for own in (slice(0, S), slice(S, P)):
                        last = nc.scalar.activation(sc_x[own, :, own], tiles(5)[own, :, own], ACT.Copy, scale=X_SCALE)
                    last.then_inc(sx_ok, 1)
                if soften:
                    g, gj, gp = soften
                    act.wait_ge(vbias_ok, g + 1)
                    exps(1, ev, gp).then_inc(ev_ok, 1)
                if turn:
                    g, gj, gp = turn
                    act.wait_ge(x2T_ps, g + 1)
                    if later(g, 2):
                        act.wait_ge(stored[gp], 32 * gj)
                    nc.scalar.activation(x2T[gp][:, :], bank[7][:, :], ACT.Copy).then_inc(x2T_ok, 1)

            steps(act, step, FIRST, STAGES, split_hi)
            act.wait_ge(w2_ld, 16 * (E + 1))

        @block.vector
        def _(dve):
            st_turn = [Turns(dve, st_ok[n], f"n_st{n}", 5 - n) for n in range(2)]
            l_turn = Turns(dve, l_ps, "n_l", 2)
            vs_turn = Turns(dve, vs_ok, "n_vs", 2)

            def bias(n, g, done, ok):
                dve.wait_ge(done, g + 1)
                nc.vector.scalar_tensor_tensor(kvbias[:, n, :], kvmax[:, n, :], bkv[:, n:n + 1],
                                               bkv[:, n:n + 1].broadcast_to([P, GB]),
                                               ALU.subtract, ALU.add).then_inc(ok, 1)

            def stats(n, g, y):
                dve.wait_ge(y_ok[n], g + 1)
                for t in range(GT):
                    last = nc.vector.bn_stats(st[n][:, t, :], y[:, t, :])
                last.then_inc(st_ok[n], 1)
                st_turn[n].wait(g + 1)
                for t in range(GT):
                    last = nc.vector.bn_aggr(mv[n][:, t, :], st[n][:, t, :])
                last.then_inc(mv_ok[n], 1)
                dve.wait_ge(mv_ok[n], g + 1)
                nc.vector.tensor_scalar(ve[n][:, :], mv[n][:, :, 1], EPS, None, ALU.add).then_inc(ve_ok[n], 1)

            def step(at):
                project, soften, mix, cross, turn, top = (at(s) for s in range(STAGES))
                if mix:
                    g, gj, gp = mix
                    dve.wait_ge(sa_ps, g + 1)
                    nc.vector.tensor_tensor(sc_a[:, :, :], tiles(4), across(mask_a[:, :], GT),
                                            ALU.mult).then_inc(sa_ok, 1)
                if soften:
                    g, gj, gp = soften
                    dve.wait_ge(v_ps, g + 1)
                    nc.vector.reduce_max(kvmax[:, 1, :], batches(3), AX.X, negate=True).then_inc(vmax_ok, 1)
                    bias(1, g, vmax_ok, vbias_ok)
                if top:
                    g, gj, gp = top
                    l_turn.wait(g + 1)
                    for t in range(GT):
                        last = nc.vector.max(vs[:, t, :], bank[7][:, t * E:(t + 1) * E])
                    last.then_inc(vs_ok, 1)
                    vs_turn.wait(g + 1)
                    for t in range(GT):
                        last = nc.vector.max_index(ix[:, t, :], vs[:, t, :], bank[7][:, t * E:(t + 1) * E])
                    last.then_inc(ix_ok, 1)
                    dve.wait_ge(ix_ok, g + 1)
                    nc.vector.tensor_copy(top_v[:, ds(g * GT, GT), :], vs[:, :, :])
                    nc.vector.tensor_copy(top_i[:, ds(g * GT, GT), :], ix[:, :, 0:K]).then_inc(top_ok, 1)
                if mix:
                    g, gj, gp = mix
                    dve.wait_ge(o1_ps, g + 1)
                    dve.wait_ge(r_ld[gp], 16 * (gj + 1))
                    if later(g, 1):
                        dve.wait_ge(xn_ok[0], g)
                    for t in range(GT):
                        last = nc.vector.scalar_tensor_tensor(y1[:, t, :], tiles(4)[:, t, :], rsum[gp][:, t:t + 1],
                                                              x_res[gp][:, t, :], ALU.mult, ALU.add)
                    last.then_inc(y_ok[0], 1)
                if mix:
                    g, gj, gp = mix
                    stats(0, g, y1)
                if project:
                    g, gj, gp = project
                    dve.wait_ge(q_ps, g + 1)
                    nc.vector.reduce_max(nmax[:, :], tiles(1), AX.X, negate=True).then_inc(qmax_ok, 1)
                if soften:
                    g, gj, gp = soften
                    dve.wait_ge(ev_ok, g + 1)
                    nc.vector.reciprocal(rsum[gp][:, :], sums[gp][:, :]).then_inc(rsum_ok, 1)
                    dve.wait_ge(rsum_ok, g + 1)
                    dve.wait_ge(qT_ps, g + 1)
                    nc.vector.tensor_tensor(qT[gp][:, :].rearrange("p (b s) -> p b s", b=GB), batches(0),
                                            over(rsum[gp][:, GT:GT + GB], S), ALU.mult).then_inc(qT_ok, 1)
                if project:
                    g, gj, gp = project
                    dve.wait_ge(k_ps, g + 1)
                    nc.vector.reduce_max(kvmax[:, 0, :], batches(2), AX.X, negate=True).then_inc(kmax_ok, 1)
                if cross:
                    g, gj, gp = cross
                    dve.wait_ge(o2_ps, g + 1)
                    if later(g, 1):
                        dve.wait_ge(xn_ok[1], g)
                    nc.vector.tensor_tensor(y2[:, :, :], tiles(6), x1[gp][:, :, :], ALU.add).then_inc(y_ok[1], 1)
                if project:
                    g, gj, gp = project
                    bias(0, g, kmax_ok, kbias_ok)
                if cross:
                    g, gj, gp = cross
                    stats(1, g, y2)

            def split_lo(n):
                dve.wait_ge(hi_ok, n + 1)
                nc.vector.tensor_tensor(w_lo[:, n, :, :], w_in[n % 2][:, :, :], w_hi[:, n, :, :].bitcast(F32),
                                        ALU.subtract).then_inc(lo_ok, 1)

            steps(dve, step, FIRST, STAGES, split_lo)


N_CONSTS = 8


def routing(nc, sem, bank, m):
    w_hi, w_lo, w2, ident = m["w_hi"], m["w_lo"], m["w2"], m["ident"]
    x2_all, x2_rows, x2T_cols, group_rows = m["x2_all"], m["x2_rows"], m["x2T_cols"], m["group_rows"]
    top_v, top_i, gates = m["top_v"], m["top_i"], m["gates"]
    src_tab, dst_tab, w_at = m["src_tab"], m["dst_tab"], m["w_at"]
    stack = ExitStack()
    with stack:
        def sb(name, shape, dt=F32):
            return stack.enter_context(nc.sbuf_tensor(name, shape, dt))

        NK = NT * K
        OH = GT * K
        OC = OH // FC
        iota_e, before_m, ones_bf, ones_f = m["iota_e"], m["before_m"], m["ones_bf"], m["ones_f"]
        iota_row, iota_blk, first_slot = m["iota_row"], m["iota_blk"], m["first_slot"]
        unused_row, tile_no, row_code = m["unused_row"], m["tile_no"], m["row_code"]
        e8 = sb("e8", [P, NT, 8])
        den = sb("den", [P, NT])
        rden = sb("rden", [P, NT])
        pick = [sb(f"pick{k}", [P, NT, E]) for k in range(K)]
        both = sb("both", [P, NT, E], BF16)
        cnt = sb("cnt", [P, E])
        cnt_i = [sb(f"cnt_i{n}", [P, E], I32) for n in range(2)]
        padded = sb("padded", [P, E])
        end = sb("end", [P, E])
        start = sb("start", [P, E])
        upto = sb("upto", [P, NT, E])
        pos = [sb(f"pos{n}", [P, NT, E]) for n in range(2)]
        slot = sb("slot", [P, NT, K])
        slot_i = sb("slot_i", [P, NK], I32)
        slot_b = sb("slot_b", [P, NK], I32)
        slot_r = sb("slot_r", [P, NK], I32)
        blk = sb("blk", [P, NK])
        row = sb("row", [P, NK])
        own = [sb(f"own{n}", [P, NB]) for n in range(2)]
        oh_row = [sb(f"oh_row{n}", [P, P], BF16) for n in range(4)]
        oh_blk = [sb(f"oh_blk{n}", [P, 2, NB], BF16) for n in range(4)]
        sg = [sb(f"sg{n}", [P, GN]) for n in range(2)]
        hT = [sb(f"hT{n}", [P, GN]) for n in range(2)]
        h_hi = [sb(f"h_hi{n}", [P, GN], F32R) for n in range(FC)]
        h_lo = [sb(f"h_lo{n}", [P, GN], F32R) for n in range(FC)]
        tab = [sb(f"tab{n}", [P, NB]) for n in range(5)]
        x2T = sb("r_x2T", [P, GN])
        w2_hi = sb("w2_hi", [P, F], F32R)
        w2_lo = sb("w2_lo", [P, F], F32R)
        sT = sb("sT", [P, GN])
        x_hi = [sb(f"r_x_hi{n}", [P, GN], F32R) for n in range(2)]
        x_lo = [sb(f"r_x_lo{n}", [P, GN], F32R) for n in range(2)]

        x_ld = sem("r_x_ld")
        all_ld = sem("r_all_ld")
        x_hi_ok = sem("r_x_hi_ok")
        x_lo_ok = sem("r_x_lo_ok")
        h_hi_ok = sem("r_h_hi_ok")
        h_lo_ok = sem("r_h_lo_ok")
        h_used = sem("r_h_used")
        w2_hi_ok = sem("r_w2_hi_ok")
        w2_lo_ok = sem("r_w2_lo_ok")
        sT_ok = sem("r_sT_ok")
        s_ps = sem("r_s_ps")
        exp_in = sem("r_exp_in")
        exp_ok = sem("r_exp_ok")
        both_ok = sem("r_both_ok")
        ranks_ps = sem("r_ranks_ps")
        pos_ok = sem("r_pos_ok")
        oh_ok = sem("r_oh_ok")
        oh_used = sem("r_oh_used")
        g_ps = sem("r_g_ps")
        u_ps = sem("r_u_ps")
        sg_ok = sem("r_sg_ok")
        hT_ok = sem("r_hT_ok")
        added = sem("r_added")
        dve_self = sem("r_dve_self")

        def table(ap):
            return ap[:, :].rearrange("p (t e) -> p t e", e=E)

        block = stack.enter_context(nc.Block())

        def groups(engine, step):
            for g in range(2):
                step(g, 0, g, True)
            with engine.Fori(1, NG // 2 - 1) as j:
                for par in range(2):
                    step(j * 2 + par, j, par, False)
            for g in range(NG - 2, NG):
                step(g, g // 2, g % 2, False)

        @block.sync
        def _(sp):
            def step(g, j, par, first):
                if not (first and par == 0):
                    sp.wait_ge(x_lo_ok, g)
                sp.dma_start(x2T[:, :], x2T_cols[:, ds(g * GN, GN)]).then_inc(x_ld, 16)
                sp.dma_start(x2_all[:, ds(g * GT, GT), :], group_rows(x2_rows, g)).then_inc(all_ld, 16)

            groups(sp, step)

        @block.gpsimd
        def _(pool):
            def x_low(g, par):
                pool.wait_ge(x_hi_ok, g + 1)
                nc.gpsimd.tensor_tensor(x_lo[par][:, :], x2T[:, :], x_hi[par][:, :].bitcast(F32),
                                        ALU.subtract).then_inc(x_lo_ok, 1)

            def h_low(n, c):
                pool.wait_ge(h_hi_ok, n + 1)
                nc.gpsimd.tensor_tensor(h_lo[c][:, :], hT[c % 2][:, :], h_hi[c][:, :].bitcast(F32),
                                        ALU.subtract).then_inc(h_lo_ok, 1)

            def step(g, j, par, first):
                for c in range(FC):
                    if not (first and par == 0 and c == 0):
                        h_low(g * FC + c - 1, (c - 1) % FC)
                    if c == 1 and (not isinstance(g, int) or g + 1 < NG):
                        x_low(g + 1, 1 - par)

            nc.gpsimd.tensor_tensor(e8[:, :, :], top_v[:, :, :], over(top_v[:, :, 0], 8),
                                    ALU.subtract).then_inc(exp_in, 1)
            x_low(0, 0)
            pool.wait_ge(w2_hi_ok, 1)
            nc.gpsimd.tensor_tensor(w2_lo[:, :], w2[:, SHARED, :], w2_hi[:, :].bitcast(F32),
                                    ALU.subtract).then_inc(w2_lo_ok, 1)
            groups(pool, step)
            h_low(NG * FC - 1, FC - 1)

        @block.tensor
        def _(pe):
            pe.wait_ge(both_ok, 1)
            flat = both[:, :, :].rearrange("p t e -> p (t e)")
            nc.tensor.matmul(bank[6][:, :], before_m[:, :], flat, start=True, stop=True)
            nc.tensor.matmul(bank[7][:, :], ones_bf[:, :], flat, start=True, stop=True).then_inc(ranks_ps, 1)

            def rows(g, par, c, early=False):
                pe.wait_ge(h_lo_ok, g * FC + c + 1)
                if c == 0 and not early:
                    pe.wait_ge(sT_ok, g - 1)
                to, w = bank[4 + par][:, :], slice(c * D, (c + 1) * D)
                nc.tensor.matmul(to, w2_hi[:, w], h_hi[c][:, :], start=(c == 0), stop=False)
                nc.tensor.matmul(to, w2_hi[:, w], h_lo[c][:, :], start=False, stop=False)
                nc.tensor.matmul(to, w2_lo[:, w], h_hi[c][:, :], start=False, stop=(c == FC - 1)).then_inc(h_used, 1)

            def back(g, early=False):
                pe.wait_ge(sT_ok, g + 1)
                if not early:
                    pe.wait_ge(added, g)
                for t in range(GT):
                    last = nc.tensor.transpose(bank[7][:, t * P:(t + 1) * P], sT[:, t * P:(t + 1) * P], ident[:, :])
                last.then_inc(s_ps, 1)

            def table_of(n, c, start):
                for q in range(c * OC, (c + 1) * OC):
                    pe.wait_ge(oh_ok, n * OC + q % OC + 1)
                    nc.tensor.matmul(bank[6][:, 0:2 * NB], oh_row[q % 4][:, :],
                                     oh_blk[q % 4][:, :, :].rearrange("p a n -> p (a n)"),
                                     start=start and q == 0, stop=True, skip_group_check=True).then_inc(oh_used, 1)

            def step(g, j, par, first):
                pe.wait_ge(x_lo_ok, g + 1)
                for c in range(FC):
                    n = g * FC + c
                    for ps, done, k, b in ((g_ps, sg_ok, 0, 0), (u_ps, hT_ok, 1, 2)):
                        if not (first and par == 0 and c < 2):
                            pe.wait_ge(done, n - 1)
                        to, w = bank[b + c % 2][:, :], slice(c * P, (c + 1) * P)
                        nc.tensor.matmul(to, w_hi[:, SHARED, k, w], x_hi[par][:, :], start=True, stop=False)
                        nc.tensor.matmul(to, w_hi[:, SHARED, k, w], x_lo[par][:, :], start=False, stop=False)
                        nc.tensor.matmul(to, w_lo[:, SHARED, k, w], x_hi[par][:, :], start=False,
                                         stop=True).then_inc(ps, 1)
                    if c >= 2:
                        rows(g, par, c - 2, first)
                    elif not (first and par == 0):
                        rows(g - 1, 1 - par, c + FC - 2)
                    if not (first and par == 0 and c == 0):
                        table_of(n - 1, (c - 1) % FC, first and par == 0 and c == 1)
                    if c == 2 and not (first and par == 0):
                        back(g - 1, first)

            groups(pe, step)
            table_of(NG * FC - 1, FC - 1, False)
            for c in range(FC - 2, FC):
                rows(NG - 1, 1, c)
            back(NG - 1)

        @block.scalar
        def _(act):
            act.wait_ge(exp_in, 1)
            nc.scalar.activation(e8[:, :, :], e8[:, :, :], ACT.Exp).then_inc(exp_ok, 1)

            def take(g, par):
                act.wait_ge(h_used, (g + 1) * FC)
                nc.scalar.activation(sT[:, :], bank[4 + par][:, :], ACT.Copy).then_inc(sT_ok, 1)

            def x_high(g, par):
                act.wait_ge(x_ld, 16 * (g + 1))
                nc.scalar.activation(x_hi[par][:, :], x2T[:, :], ACT.Copy).then_inc(x_hi_ok, 1)

            def h_high(n, c, early):
                act.wait_ge(hT_ok, n + 1)
                if not early:
                    act.wait_ge(h_used, n - FC + 1)
                nc.scalar.activation(h_hi[c][:, :], hT[c % 2][:, :], ACT.Copy).then_inc(h_hi_ok, 1)

            def step(g, j, par, first):
                for c in range(FC):
                    n = g * FC + c
                    act.wait_ge(g_ps, n + 1)
                    if not (first and par == 0 and c < 2):
                        act.wait_ge(hT_ok, n - 1)
                    nc.scalar.activation(sg[c % 2][:, :], bank[c % 2][:, :], ACT.Silu).then_inc(sg_ok, 1)
                    if not (first and par == 0 and c == 0):
                        h_high(n - 1, (c - 1) % FC, first and (par == 0 or c == 0))
                    if c == 1 and (not isinstance(g, int) or g + 1 < NG):
                        x_high(g + 1, 1 - par)
                    if c == 1 and not (first and par == 0):
                        take(g - 1, 1 - par)

            x_high(0, 0)
            nc.scalar.activation(w2_hi[:, :], w2[:, SHARED, :], ACT.Copy).then_inc(w2_hi_ok, 1)
            groups(act, step)
            h_high(NG * FC - 1, FC - 1, False)
            take(NG - 1, 1)

        @block.vector
        def _(dve):
            c = Done(dve, dve_self)
            for k in range(K):
                c.add(nc.vector.tensor_tensor(pick[k][:, :, :], across(iota_e[:, :], NT), over(top_i[:, :, k], E),
                                              ALU.is_equal))
            c.wait()
            nc.vector.tensor_tensor(both[:, :, :], pick[0][:, :, :], pick[1][:, :, :], ALU.add).then_inc(both_ok, 1)
            dve.wait_ge(ranks_ps, 1)
            c.link(nc.vector.reduce_sum(cnt[:, :], table(bank[7]).rearrange("p t e -> p e t"), AX.X))
            c.link(nc.vector.tensor_scalar(cnt_i[0][:, :], cnt[:, :], float(P - 1), None, ALU.add))
            shift = P.bit_length() - 1
            c.link(nc.vector.tensor_scalar(cnt_i[1][:, :], cnt_i[0][:, :], shift, shift,
                                           ALU.logical_shift_right, ALU.logical_shift_left))
            c.link(nc.vector.tensor_copy(padded[:, :], cnt_i[1][:, :]))
            c.link(nc.vector.tensor_tensor_scan(end[:, :], ones_f[:, 0:E], padded[:, :], 0.0, ALU.mult, ALU.add))
            c.link(nc.vector.tensor_tensor(start[:, :], end[:, :], padded[:, :], ALU.subtract))
            for e in range(E):
                c.add(nc.vector.tensor_tensor_scan(upto[:, :, e], ones_f[:, :], table(bank[7])[:, :, e],
                                                   start[:, e:e + 1], ALU.mult, ALU.add))
            c.wait()
            c.link(nc.vector.tensor_tensor(pos[0][:, :, :], table(bank[7]), upto[:, :, :], ALU.subtract))
            nc.vector.tensor_tensor(pos[1][:, :, :], table(bank[6]), pos[0][:, :, :],
                                    ALU.subtract).then_inc(pos_ok, 1)
            dve.wait_ge(pos_ok, 1)
            for k in range(K):
                c.link(nc.vector.tensor_tensor(pos[0][:, :, :], pick[k][:, :, :], pos[1][:, :, :], ALU.mult))
                c.link(nc.vector.reduce_sum(slot[:, :, k], pos[0][:, :, :], AX.X))
            c.link(nc.vector.tensor_copy(slot_i[:, :], slot[:, :, :].rearrange("p t k -> p (t k)")))
            c.add(nc.vector.tensor_scalar(slot_b[:, :], slot_i[:, :], shift, None, ALU.logical_shift_right))
            c.add(nc.vector.tensor_scalar(slot_r[:, :], slot_i[:, :], P - 1, None, ALU.bitwise_and))
            c.wait()
            c.add(nc.vector.tensor_copy(blk[:, :], slot_b[:, :]))
            c.add(nc.vector.tensor_copy(row[:, :], slot_r[:, :]))
            c.wait()
            assert c.n == R_SELF

            def one_hots(g, c, first):
                for q in range(c * OC, (c + 1) * OC):
                    n = g * OH + q
                    if not (first and q < 4):
                        dve.wait_ge(oh_used, n - 3)
                    nc.vector.tensor_scalar(oh_row[q % 4][:, :], iota_row[:, :], row[:, ds(n, 1)], None, ALU.is_equal)
                    nc.vector.tensor_scalar(oh_blk[q % 4][:, 0, :], iota_blk[:, :], blk[:, ds(n, 1)],
                                            row_code[:, q % K:q % K + 1], ALU.is_equal, ALU.mult)
                    nc.vector.tensor_scalar(oh_blk[q % 4][:, 1, :], iota_blk[:, :], blk[:, ds(n, 1)],
                                            tile_no[:, ds(g * GT + q // K, 1)], ALU.is_equal, ALU.mult
                                            ).then_inc(oh_ok, 1)

            def add(g):
                dve.wait_ge(all_ld, 16 * (g + 1))
                dve.wait_ge(s_ps, g + 1)
                at = x2_all[:, ds(g * GT, GT), :].rearrange("p t d -> p (t d)")
                nc.vector.scalar_tensor_tensor(at, bank[7][:, :], ALPHA / NS, at, ALU.mult,
                                               ALU.add).then_inc(added, 1)

            def aside(n):
                if n == 0:
                    dve.wait_ge(exp_ok, 1)
                    c.add(nc.vector.reduce_sum(den[:, :], e8[:, :, :], AX.X))
                if n == 1:
                    c.wait()
                    c.add(nc.vector.reciprocal(rden[:, :], den[:, :]))
                    c.add(nc.vector.memset(own[0][:, :], 0.0))
                if n == 2:
                    c.wait()
                    for k in range(K):
                        c.add(nc.vector.scalar_tensor_tensor(gates[:, k, :], rden[:, :], 1.0 - ALPHA, e8[:, :, k],
                                                             ALU.mult, ALU.mult))
                if n >= 1:
                    e = n - 1
                    c.wait()
                    c.add(nc.vector.scalar_tensor_tensor(own[(e + 1) % 2][:, :], first_slot[:, :], end[:, e:e + 1],
                                                         own[e % 2][:, :], ALU.is_ge, ALU.add))

            def step(g, j, par, first):
                for c in range(FC):
                    n = g * FC + c
                    dve.wait_ge(sg_ok, n + 1)
                    dve.wait_ge(u_ps, n + 1)
                    if not (first and par == 0 and c < 2):
                        dve.wait_ge(h_lo_ok, n - 1)
                    nc.vector.tensor_tensor(hT[c % 2][:, :], sg[c % 2][:, :], bank[2 + c % 2][:, :],
                                            ALU.mult).then_inc(hT_ok, 1)
                    one_hots(g, c, first and par == 0)
                    if c == 2 and not (first and par == 0):
                        add(g - 1)
                    if isinstance(g, int) and g >= NG - 2:
                        aside((g - NG + 2) * FC + c)

            groups(dve, step)
            c.wait()
            c.add(nc.vector.tensor_scalar(w_at[:, :], own[(E - 1) % 2][:, :], float(F), None, ALU.mult))
            code, empty, less, moved, src = tab
            dve.wait_ge(oh_used, NK)
            c.link(nc.vector.tensor_scalar(code[:, :], bank[6][:, NB:2 * NB], float(K * P), None, ALU.mult))
            c.link(nc.vector.tensor_tensor(less[:, :], bank[6][:, 0:NB], code[:, :], ALU.add))
            c.add(nc.vector.tensor_scalar(empty[:, :], less[:, :], 0.0, None, ALU.is_equal))
            c.add(nc.vector.tensor_scalar(src[:, :], less[:, :], 1.0, 0.0, ALU.subtract, ALU.max))
            c.wait()
            c.link(nc.vector.tensor_tensor(moved[:, :], empty[:, :], unused_row[:, :], ALU.mult))
            c.link(nc.vector.scalar_tensor_tensor(code[:, :], less[:, :], -1.0, moved[:, :], ALU.add, ALU.add))
            c.add(nc.vector.tensor_copy(dst_tab[:, :], code[:, :]))
            c.link(nc.vector.tensor_copy(src_tab[:, :], src[:, :]))
            c.link(nc.vector.tensor_scalar(src_tab[:, :], src_tab[:, :], K.bit_length() - 1, None,
                                           ALU.logical_shift_right))
            add(NG - 1)


R_SELF = 2 + 6 + E + 1 + 2 * K + 1 + 4


def experts(nc, sem, bank, m):
    w_hi, w_lo, w2, ident = m["w_hi"], m["w_lo"], m["w2"], m["ident"]
    src_tab, dst_tab, w_at = m["src_tab"], m["dst_tab"], m["w_at"]
    x2_rows, y_rows = m["x2_rows"], m["y_rows"]
    stack = ExitStack()
    with stack:
        def sb(name, shape, dt=F32):
            return stack.enter_context(nc.sbuf_tensor(name, shape, dt))

        src = [sb(f"src{n}", [P, 1], U32) for n in range(2)]
        dst = [sb(f"dst{n}", [P, 1], U32) for n in range(2)]
        xg = [sb(f"xg{n}", [P, D]) for n in range(2)]
        x_hi = [sb(f"e_x_hi{n}", [P, P], F32R) for n in range(2)]
        x_lo = [sb(f"e_x_lo{n}", [P, P], F32R) for n in range(2)]
        sg = [sb(f"e_sg{n}", [P, F]) for n in range(2)]
        h = [sb(f"e_h{n}", [P, F]) for n in range(2)]
        hT = [sb(f"e_hT{n}", [P, F]) for n in range(2)]
        y = [sb(f"e_y{n}", [P, D]) for n in range(2)]

        src_ok = sem("e_src_ok")
        gathered = [sem(f"e_gathered{n}") for n in range(2)]
        scattered = [sem(f"e_scattered{n}") for n in range(2)]
        xT_ps = sem("e_xT_ps")
        x_hi_ok = sem("e_x_hi_ok")
        x_lo_ok = sem("e_x_lo_ok")
        g_ps = sem("e_g_ps")
        u_ps = sem("e_u_ps")
        sg_ok = sem("e_sg_ok")
        h_ok = sem("e_h_ok")
        hT_ps = sem("e_hT_ps")
        hT_ok = sem("e_hT_ok")
        y_ps = sem("e_y_ps")
        y_ok = sem("e_y_ok")

        block = stack.enter_context(nc.Block())

        def steps(engine, step):
            for b in range(6):
                step(b, b // 2, b % 2)
            with engine.Fori(3, NB // 2 - 2) as j:
                for par in range(2):
                    step(j * 2 + par, j, par, inner=True)
            for b in range(NB - 4, NB + 3):
                step(b, b // 2, b % 2)

        @block.gpsimd
        def _(pool):
            src_turn = Turns(pool, src_ok, "n_src", 6 + 3 + 1)
            y_turn = Turns(pool, y_ok, "n_y", 3 + 1)

            def gather(b, par):
                src_turn.wait(b + 1)
                nc.gpsimd.indirect_dma_start(xg[par][:, :], None, x2_rows,
                                             bass.IndirectOffsetOnAxis(src[par][:, 0:1], 0)
                                             ).then_inc(gathered[par], 16)

            def scatter(b, par):
                y_turn.wait(b + 1)
                nc.gpsimd.indirect_dma_start(y_rows, bass.IndirectOffsetOnAxis(dst[par][:, 0:1], 0),
                                             y[par][:, :], None).then_inc(scattered[par], 16)

            for b in range(3):
                gather(b, b % 2)

            def step(b, j, par, inner=False):
                if inner or b >= 3:
                    scatter(b - 3, 1 - par)
                if inner or b + 3 < NB:
                    gather(b + 3, 1 - par)

            steps(pool, step)
            for n in range(2):
                pool.wait_ge(scattered[n], 16 * (NB // 2))

        @block.tensor
        def _(pe):
            at_reg = [pe.alloc_register(f"w_at{n}") for n in range(2)]
            w2_at_reg = [pe.alloc_register(f"w2_at{n}") for n in range(2)]

            def look_up(b, par):
                pe.reg_load(at_reg[par], w_at[0:1, ds(b, 1)])

            def weights_at(regs, par):
                return pe.snap(regs[par], min_val=0, max_val=(E - 1) * F)

            def product(to, x, at):
                def columns(w):
                    return w[:, :, :, :].rearrange("p e k f -> p (e k f)")[:, ds(at, F)]

                nc.tensor.matmul(to, x[0], columns(w_hi), start=True, stop=False)
                nc.tensor.matmul(to, x[1], columns(w_hi), start=False, stop=False)
                return nc.tensor.matmul(to, x[0], columns(w_lo), start=False, stop=True)

            def transpose_x(par, gathers):
                pe.wait_ge(gathered[par], 16 * gathers)
                nc.tensor.transpose(bank[7][:, 0:P], xg[par][:, :], ident[:, :]).then_inc(xT_ps, 1)

            look_up(0, 0)
            transpose_x(0, 1)

            def step(b, j, par, inner=False):
                other = 1 - par
                if inner or b < NB:
                    at = weights_at(at_reg, par)
                    pe.wait_ge(x_lo_ok, b + 1)
                    x = (x_hi[par][:, :], x_lo[par][:, :])
                    if inner or b >= 2:
                        pe.wait_ge(sg_ok, b - 1)
                    product(bank[par][:, :], x, at * 2).then_inc(g_ps, 1)
                if inner or b + 1 < NB:
                    look_up(b + 1, other)
                    transpose_x(other, j + 1 + par)
                if inner or 1 <= b <= NB:
                    pe.wait_ge(h_ok, b)
                    for c in range(FC):
                        last = nc.tensor.transpose(bank[4 + other][:, c * P:(c + 1) * P],
                                                   h[other][:, c * P:(c + 1) * P], ident[:, :])
                    last.then_inc(hT_ps, 1)
                if inner or b < NB:
                    product(bank[2 + par][:, :], x, at * 2 + F).then_inc(u_ps, 1)
                if inner or 2 <= b <= NB + 1:
                    before = weights_at(w2_at_reg, par)
                    pe.wait_ge(hT_ok, b - 1)
                    if inner or b >= 3:
                        pe.wait_ge(y_ok, b - 2)
                    for c in range(FC):
                        last = nc.tensor.matmul(bank[6][:, 0:D], hT[par][:, c * P:(c + 1) * P],
                                                w2[:, :, :].rearrange("p e f -> p (e f)")[:, ds(before + c * D, D)],
                                                start=(c == 0), stop=(c == FC - 1))
                    last.then_inc(y_ps, 1)
                if inner or b < NB:
                    pe.reg_mov(w2_at_reg[par], at_reg[par])

            steps(pe, step)

        @block.scalar
        def _(act):
            def x_high(b, par):
                act.wait_ge(xT_ps, b + 1)
                nc.scalar.activation(x_hi[par][:, :], bank[7][:, 0:P], ACT.Copy).then_inc(x_hi_ok, 1)

            x_high(0, 0)

            def step(b, j, par, inner=False):
                other = 1 - par
                if inner or b + 1 < NB:
                    x_high(b + 1, other)
                if inner or b < NB:
                    act.wait_ge(g_ps, b + 1)
                    if inner or b >= 2:
                        act.wait_ge(h_ok, b - 1)
                    nc.scalar.activation(sg[par][:, :], bank[par][:, :], ACT.Silu).then_inc(sg_ok, 1)
                if inner or 1 <= b <= NB:
                    act.wait_ge(hT_ps, b)
                    nc.scalar.activation(hT[other][:, :], bank[4 + other][:, :], ACT.Copy).then_inc(hT_ok, 1)

            steps(act, step)

        @block.vector
        def _(dve):
            def stage(b, par):
                nc.vector.tensor_copy(src[par][:, :], src_tab[:, ds(b, 1)]).then_inc(src_ok, 1)

            def take_x(b, par):
                dve.wait_ge(x_hi_ok, b + 1)
                nc.vector.tensor_tensor(x_lo[par][:, :], bank[7][:, 0:P], x_hi[par][:, :].bitcast(F32),
                                        ALU.subtract).then_inc(x_lo_ok, 1)

            stage(0, 0)
            stage(1, 1)
            take_x(0, 0)
            stage(2, 0)

            def step(b, j, par, inner=False):
                other = 1 - par
                if inner or b >= 3:
                    dve.wait_ge(y_ps, b - 2)
                    if inner or b >= 5:
                        dve.wait_ge(scattered[other], 16 * (j - 2 + par))
                    nc.vector.tensor_copy(dst[other][:, :], dst_tab[:, ds(b - 3, 1)])
                    nc.vector.tensor_copy(y[other][:, :], bank[6][:, 0:D]).then_inc(y_ok, 1)
                if inner or b + 1 < NB:
                    take_x(b + 1, other)
                if inner or b + 3 < NB:
                    stage(b + 3, other)
                if inner or b < NB:
                    dve.wait_ge(sg_ok, b + 1)
                    dve.wait_ge(u_ps, b + 1)
                    nc.vector.tensor_tensor(h[par][:, :], sg[par][:, :], bank[2 + par][:, :],
                                            ALU.mult).then_inc(h_ok, 1)

            steps(dve, step)


def combine(nc, sem, bank, m):
    x2_all, gates, minus_half, y_rows, out_rows = m["x2_all"], m["gates"], m["minus_half"], m["y_rows"], m["out_rows"]
    group_rows = m["group_rows"]
    stack = ExitStack()
    with stack:
        def sb(name, shape, dt=F32):
            return stack.enter_context(nc.sbuf_tensor(name, shape, dt))

        def pair(name, shape):
            return [sb(f"{name}{n}", shape) for n in range(2)]

        R = 4
        yk = [sb(f"yk{n}", [P, GT, K, D]) for n in range(R)]
        gated = [pair(f"gated{k}_", [P, GT, D]) for k in range(K)]
        part = sb("part", [P, GT, D])
        z = pair("z", [P, GT, D])
        res = pair("res", [P, GT, D])
        st = sb("f_st", [P, GT, 6])
        mv = pair("f_mv", [P, GT, 2])
        ve = pair("f_ve", [P, GT])
        rs = pair("f_rs", [P, GT])

        y_ld = [sem(f"f_y_ld{n}") for n in range(R)]
        stored = [sem(f"f_stored{n}") for n in range(2)]
        gated_ok, part_ok, z_ok, st_ok, mv_ok, ve_ok, moved_ok, res_ok = (
            sem(f"f_{n}") for n in "gated_ok part_ok z_ok st_ok mv_ok ve_ok moved_ok res_ok".split())

        block = stack.enter_context(nc.Block())
        both = y_rows[0:T * K, :].rearrange("(n k) d -> n (k d)", k=K)

        def groups(engine, step):
            for g in range(R):
                step(g, 0, g)
            with engine.Fori(1, NG // R) as j:
                for r in range(R):
                    step(j * R + r, j, r)

        def later(g, n):
            return not isinstance(g, int) or g >= n

        @block.sync
        def _(sp):
            def load(g, r):
                sp.dma_start(yk[r][:, :, :, :].rearrange("p t k d -> p t (k d)"),
                             both[ds(g * GN, GN), :].rearrange("(t p) d -> p t d", p=P)).then_inc(y_ld[r], 16)

            def store(g, par):
                sp.wait_ge(res_ok, g + 1)
                sp.dma_start(group_rows(out_rows, g), res[par][:, :, :]).then_inc(stored[par], 16)

            LAG = R + 2
            for g in range(R):
                load(g, g)
            for g in range(R, 2 * R):
                sp.wait_ge(gated_ok, g - R + 1)
                load(g, g % R)
                if g >= LAG:
                    store(g - LAG, (g - LAG) % 2)
            with sp.Fori(2, NG // R) as j:
                for r in range(R):
                    g = j * R + r
                    sp.wait_ge(gated_ok, g - R + 1)
                    load(g, r)
                    store(g - LAG, (r - LAG) % 2)
            for g in range(NG - LAG, NG):
                store(g, g % 2)
            for n in range(2):
                sp.wait_ge(stored[n], 16 * (NG // 2))

        @block.scalar
        def _(act):
            def step(g, j, r):
                act.wait_ge(y_ld[r], 16 * (j + 1))
                if later(g, 2):
                    act.wait_ge(z_ok, g - 1)
                for k in range(K):
                    for t in range(GT):
                        last = nc.scalar.activation(gated[k][r % 2][:, t, :], yk[r][:, t, k, :], ACT.Copy,
                                                    scale=gates[:, k, ds(g * GT + t, 1)])
                last.then_inc(gated_ok, 1)

            groups(act, step)

        @block.vector
        def _(dve):
            st_turn = Turns(dve, st_ok, "n_f_st", R + 1)

            def step(g, j, r):
                par = r % 2
                dve.wait_ge(gated_ok, g + 1)
                nc.vector.tensor_tensor(part[:, :, :], gated[0][par][:, :, :], gated[1][par][:, :, :],
                                        ALU.add).then_inc(part_ok, 1)
                if later(g, 2):
                    dve.wait_ge(moved_ok, g - 1)
                dve.wait_ge(part_ok, g + 1)
                nc.vector.tensor_tensor(z[par][:, :, :], part[:, :, :], x2_all[:, ds(g * GT, GT), :],
                                        ALU.add).then_inc(z_ok, 1)
                dve.wait_ge(z_ok, g + 1)
                for t in range(GT):
                    last = nc.vector.bn_stats(st[:, t, :], z[par][:, t, :])
                last.then_inc(st_ok, 1)
                st_turn.wait(g + 1)
                for t in range(GT):
                    last = nc.vector.bn_aggr(mv[par][:, t, :], st[:, t, :])
                last.then_inc(mv_ok, 1)
                dve.wait_ge(mv_ok, g + 1)
                nc.vector.tensor_scalar(ve[par][:, :], mv[par][:, :, 1], EPS, None, ALU.add).then_inc(ve_ok, 1)

            groups(dve, step)

        @block.gpsimd
        def _(pool):
            def step(g, j, r):
                par = r % 2
                pool.wait_ge(ve_ok, g + 1)
                nc.gpsimd.tensor_tensor(rs[par][:, :], ve[par][:, :], minus_half[:, 0:GT], ALU.pow)
                if later(g, 2):
                    pool.wait_ge(stored[par], 16 * (j * (R // 2) + r // 2))
                nc.gpsimd.tensor_tensor(res[par][:, :, :], z[par][:, :, :], over(mv[par][:, :, 0], D),
                                        ALU.subtract).then_inc(moved_ok, 1)
                pool.wait_ge(moved_ok, g + 1)
                nc.gpsimd.tensor_tensor(res[par][:, :, :], res[par][:, :, :], over(rs[par][:, :], D),
                                        ALU.mult).then_inc(res_ok, 1)

            groups(pool, step)


_INS = ["x", "ctx_1024", "L0_attn_Wq", "L0_attn_bq", "L0_attn_Wk", "L0_attn_bk", "L0_attn_Wv", "L0_attn_bv",
        "L0_ffn_gate_W", "L0_ffn_w1_e", "L0_ffn_w3_e", "L0_ffn_w2_e", "L0_ffn_w1_s", "L0_ffn_w3_s", "L0_ffn_w2_s"]


def kernel(**inputs):
    import numpy as _np
    import concourse.bacc as _bacc
    from concourse import mybir as _mybir
    from concourse.bass_utils import run_bass_kernel_spmd as _run

    nc = _bacc.Bacc("TRN2", target_bir_lowering=False, num_devices=1)
    arrays, args = {}, []
    for name in _INS:
        a = _np.ascontiguousarray(inputs[name])
        arrays[f"in_{name}_dram"] = a
        args.append(nc.dram_tensor(f"in_{name}_dram", a.shape, _mybir.dt.from_np(a.dtype), kind="ExternalInput").ap())
    out = nc.dram_tensor("out_0_dram", (B, S, D), _mybir.dt.float32, kind="ExternalOutput").ap()
    decoder(nc, *args, out)
    r = _run(nc, [arrays], core_ids=[0])
    return r.results[0]["out_0_dram"]
```
